# Optimizing a Trainium2 kernel written in Bass

```python
import numpy as np
import jax
import jax.numpy as jnp

def _softmax(x, axis=-1):
    return jax.nn.softmax(x, axis=axis)

def _gelu(x):
    return jax.nn.gelu(x, approximate=True)

def _silu(x):
    return jax.nn.silu(x)

def _sigmoid(x):
    return jax.nn.sigmoid(x)

def _layernorm(x, axis=-1, eps=1e-05):
    m = jnp.mean(x, axis=axis, keepdims=True)
    v = jnp.var(x, axis=axis, keepdims=True)
    return (x - m) / jnp.sqrt(v + eps)

def _scatter_add(tgt, idx, src, axis=0):
    return tgt.at[idx].add(src)

def _segment_sum(src, seg, n):
    return jax.ops.segment_sum(src, seg, n)
kernel_name = 'mk_vit_tower_cls_d1_tok_img768_r4_27fe65'

def setup_inputs(seed: int=0):
    np.random.seed(seed)
    _w = jnp.asarray

    def _rec_inputs():
        import jax
        import jax.numpy as jnp
        _rk = jax.random.key(seed)
        x = -0.00016672 + 0.999947 * jax.random.normal(jax.random.fold_in(_rk, 1), (64, 224, 224, 3), jnp.float32)
        cls_tok = 0.02 * jax.random.normal(jax.random.fold_in(_rk, 5), (1, 1, 192), jnp.float32)
        return (x, cls_tok)
    x, cls_tok = _rec_inputs()

    def _L0_tok_setup():
        import jax, jax.numpy as jnp
        import numpy as np
        PATCH = 16
        HIDDEN = 192

        def _patchify(x, p):
            B, H, W, C = x.shape
            gh, gw = (H // p, W // p)
            x = x.reshape(B, gh, p, gw, p, C)
            x = x.transpose(0, 1, 3, 2, 4, 5)
            return x.reshape(B, gh * gw, p * p * C)
        key = jax.random.key(seed)
        kx, kw, kb = jax.random.split(key, 3)
        B, H, W, C = (64, 96, 96, 3)
        patch_dim = PATCH * PATCH * C
        x = jax.random.normal(kx, (B, H, W, C), dtype=jnp.float32)
        limit = np.sqrt(6.0 / (patch_dim + HIDDEN)).astype(np.float32)
        W_proj = jax.random.uniform(kw, (patch_dim, HIDDEN), dtype=jnp.float32, minval=-limit, maxval=limit)
        b_proj = jnp.zeros((HIDDEN,), dtype=jnp.float32)
        return {'x': x, 'W_proj': W_proj, 'b_proj': b_proj}
    _L0_tok_all = _L0_tok_setup()
    _L0_tok_in = {k: v for k, v in _L0_tok_all.items() if k in ('W_proj', 'b_proj')}
    del _L0_tok_all

    def _L0_attn_setup():
        import jax, jax.numpy as jnp
        import numpy as np
        N_HEAD = 12
        key = jax.random.key(seed)
        k1, k2, k3 = jax.random.split(key, 3)
        B, L, D = (4, 512, 192)
        x = jax.random.normal(k1, (B, L, D), dtype=jnp.float32)
        w_attn = jax.random.normal(k2, (D, 3 * D), dtype=jnp.float32) * 0.02
        w_proj = jax.random.normal(k3, (D, D), dtype=jnp.float32) * 0.02
        b_proj = jnp.zeros((D,), dtype=jnp.float32)
        return {'x': x, 'w_attn': w_attn, 'w_proj': w_proj, 'b_proj': b_proj}
    _L0_attn_all = _L0_attn_setup()
    _L0_attn_in = {k: v for k, v in _L0_attn_all.items() if k in ('w_attn', 'w_proj', 'b_proj')}
    del _L0_attn_all

    def _L0_ffn_setup():
        import jax, jax.numpy as jnp
        import numpy as np
        B, T, H, F, E = (128, 32, 192, 768, 3)
        key = jax.random.key(seed)
        ks = jax.random.split(key, 4)
        s = 0.02
        return {'x': jax.random.normal(ks[0], (B, T, H), jnp.float32), 'Wg': jax.random.normal(ks[1], (E, H), jnp.float32) * s, 'W1': jax.random.normal(ks[2], (E, H, F), jnp.float32) * s, 'b1': jnp.zeros((E, F), jnp.float32), 'W2': jax.random.normal(ks[3], (E, F, H), jnp.float32) * s, 'b2': jnp.zeros((E, H), jnp.float32)}
    _L0_ffn_all = _L0_ffn_setup()
    _L0_ffn_in = {k: v for k, v in _L0_ffn_all.items() if k in ('Wg', 'W1', 'b1', 'W2', 'b2')}
    del _L0_ffn_all
    return {'x': x, 'cls_tok': cls_tok, 'L0_tok_W_proj': _L0_tok_in['W_proj'], 'L0_tok_b_proj': _L0_tok_in['b_proj'], 'L0_attn_w_attn': _L0_attn_in['w_attn'], 'L0_attn_w_proj': _L0_attn_in['w_proj'], 'L0_attn_b_proj': _L0_attn_in['b_proj'], 'L0_ffn_Wg': _L0_ffn_in['Wg'], 'L0_ffn_W1': _L0_ffn_in['W1'], 'L0_ffn_b1': _L0_ffn_in['b1'], 'L0_ffn_W2': _L0_ffn_in['W2'], 'L0_ffn_b2': _L0_ffn_in['b2']}

def reference(x, cls_tok, L0_tok_W_proj, L0_tok_b_proj, L0_attn_w_attn, L0_attn_w_proj, L0_attn_b_proj, L0_ffn_Wg, L0_ffn_W1, L0_ffn_b1, L0_ffn_W2, L0_ffn_b2):
    import jax
    import jax.numpy as jnp

    def _L0_tok_ref(x, W_proj, b_proj):
        import jax, jax.numpy as jnp
        import numpy as np
        PATCH = 16
        HIDDEN = 192

        def _patchify(x, p):
            B, H, W, C = x.shape
            gh, gw = (H // p, W // p)
            x = x.reshape(B, gh, p, gw, p, C)
            x = x.transpose(0, 1, 3, 2, 4, 5)
            return x.reshape(B, gh * gw, p * p * C)
        patches = _patchify(x, PATCH)
        return jnp.einsum('bnd,dh->bnh', patches, W_proj) + b_proj

    def _L0_attn_ref(x, w_attn, w_proj, b_proj):
        import jax, jax.numpy as jnp
        import numpy as np
        N_HEAD = 12
        B, L, D = x.shape
        hd = D // N_HEAD
        qkv = x @ w_attn
        q, k, v = jnp.split(qkv, 3, axis=-1)
        q = q.reshape(B, L, N_HEAD, hd).transpose(0, 2, 1, 3)
        k = k.reshape(B, L, N_HEAD, hd).transpose(0, 2, 1, 3)
        v = v.reshape(B, L, N_HEAD, hd).transpose(0, 2, 1, 3)
        scores = jnp.einsum('bhqd,bhkd->bhqk', q, k) * (1.0 / jnp.sqrt(jnp.float32(hd)))
        causal = jnp.tril(jnp.ones((L, L), dtype=bool))
        scores = jnp.where(causal[None, None, :, :], scores, -jnp.inf)
        attn = jax.nn.softmax(scores, axis=-1)
        out = jnp.einsum('bhqk,bhkd->bhqd', attn, v)
        out = out.transpose(0, 2, 1, 3).reshape(B, L, D)
        return out @ w_proj + b_proj

    def _L0_ffn_ref(x, Wg, W1, b1, W2, b2):
        import jax, jax.numpy as jnp
        import numpy as np
        B, T, H, F, E = (128, 32, 192, 768, 3)
        scores = jax.nn.softmax(jnp.mean(x, axis=1) @ Wg.T, axis=-1)
        _, idx = jax.lax.top_k(scores, 1)
        sel = idx[:, 0]
        h = jax.nn.gelu(jnp.einsum('bth,ehf->betf', x, W1) + b1[None, :, None, :], approximate=False)
        y = jnp.einsum('betf,efh->beth', h, W2) + b2[None, :, None, :]
        w = scores * jax.nn.one_hot(sel, E, dtype=scores.dtype)
        out = jnp.einsum('beth,be->bth', y, w)
        return out
    h = _L0_tok_ref(x, L0_tok_W_proj, L0_tok_b_proj)
    h = jnp.concatenate([jnp.broadcast_to(cls_tok, (h.shape[0], 1, h.shape[2])), h], axis=1)
    h = h + _L0_attn_ref(_layernorm(h, axis=-1), L0_attn_w_attn, L0_attn_w_proj, L0_attn_b_proj)
    h = h + _L0_ffn_ref(_layernorm(h, axis=-1), L0_ffn_Wg, L0_ffn_W1, L0_ffn_b1, L0_ffn_W2, L0_ffn_b2)
    return h

_drawn_inputs = setup_inputs


def setup_inputs(seed=0):
    import zlib

    import numpy as np

    out = dict(_drawn_inputs(seed))
    spreads = {'L0_tok_b_proj': (0.0, 0.1),
     'L0_attn_b_proj': (0.0, 0.1),
     'L0_ffn_b1': (0.0, 0.8),
     'L0_ffn_b2': (0.0, 0.297)}
    factors = {'cls_tok': 7.376, 'L0_attn_w_attn': 3.993, 'L0_attn_w_proj': 3.765}
    for name, (base, spread) in spreads.items():
        noise = np.random.default_rng([zlib.crc32(name.encode()), seed]).standard_normal(out[name].shape)
        drawn = base * np.exp(spread * noise) if base else spread * noise
        out[name] = jnp.asarray(drawn.astype(out[name].dtype))
    for name, factor in factors.items():
        out[name] = (out[name] * factor).astype(out[name].dtype)
    return out
```

```python
import concourse.bass as bass
from concourse import mybir
from contextlib import ExitStack

F32 = mybir.dt.float32
F32R = mybir.dt.float32r
BF16 = mybir.dt.bfloat16
I32 = mybir.dt.int32
ALU = mybir.AluOpType
ACT = mybir.ActivationFunctionType
AX_X = mybir.AxisListType.X

IMAGES, GRID, PATCH, CH = 64, 14, 16, 3
HID, HEADS, EXPERTS, FFN = 192, 12, 3, 768
HD = HID // HEADS
TOKENS = GRID * GRID + 1
PAD = TOKENS + 1
TILE = PAD // 2
PD = PATCH * PATCH * CH
KP = PD // 128
HALF = HID // 2
HPC = HEADS // 2
FCH = FFN // 128
GROUPS = HEADS // 4
KEYS0 = TILE + 1
PCOLS = PAD + KEYS0
MROW = 96
EPS = 1e-5
BIG = -1e30
W2COLS = FCH * HID + FCH


class Image:

    def __init__(self, first, trip=None):
        self.first, self.trip = first, trip
        self.par = first % 2

    def count(self, per, more):
        c = per * self.first + more
        return c if self.trip is None else self.trip * (2 * per) + c

    def turns(self, per, more):
        c = per * (self.first // 2) + more
        return c if self.trip is None else self.trip * per + c

    def back(self, k):
        return Image(self.first - k, self.trip)

    def real(self):
        return self.trip is not None or 0 <= self.first < IMAGES

    def index(self):
        return self.first if self.trip is None else self.trip * 2 + self.first


class BankTurns:

    def __init__(self, pe):
        self.pe, self.last, self.trip = pe, {}, None

    def take(self, bank, image, read_done, per, more):
        if bank in self.last:
            sem, p, m, first = self.last[bank]
            self.pe.wait_ge(sem, Image(first, self.trip).count(p, m))
        self.last[bank] = (read_done, per, more, image.first)

    def leave(self, trips):
        self.last = {b: (s, p, m, f + 2 * (trips - 1)) for b, (s, p, m, f) in self.last.items()}
        self.trip = None


def run_turns(engine, turn, enter=None, leave=None):
    for n in range(-1, 3):
        turn(n, None)
    trips = (IMAGES - 6) // 2
    with engine.Fori(0, trips) as trip:
        if enter:
            enter(trip)
        turn(3, trip)
        turn(4, trip)
    if leave:
        leave(trips)
    for n in range(3 + 2 * trips, IMAGES + 2):
        turn(n, None)


def vit_tower(nc, x, tok_w, tok_bias, attn_w, proj_bias, gate_w, w1, w2b1, b2, out):
    ctx = ExitStack()
    with ctx:
        def sb(name, shape, dt=F32):
            return ctx.enter_context(nc.sbuf_tensor(name, shape, dt))

        def two(name, shape, dt=F32):
            return [sb(f"{name}{i}", shape, dt) for i in range(2)]

        def sem(name):
            return ctx.enter_context(nc.semaphore(name))

        w1_split = nc.dram_tensor("w1_split", [EXPERTS, HALF, 4 * FFN], F32, kind="Internal").ap()

        ident = sb("ident", [128, 128])
        ident_b = sb("ident_b", [TILE, TILE], BF16)
        causal0 = sb("causal0", [TILE, KEYS0], BF16)
        causal1 = sb("causal1", [TILE, KEYS0], BF16)
        head_rows = sb("head_rows", [HALF, HPC])
        pick_max = sb("pick_max", [128, HPC])
        real_tok = sb("real_tok", [TILE, 2])
        ones_row = sb("ones_row", [1, TILE])
        minus_half = sb("minus_half", [TILE, 2])
        tok_w_sb = sb("tok_w_sb", [128, KP, HID])
        tok_bias_sb = sb("tok_bias_sb", [TILE, 2, HID])
        proj_bias_sb = sb("proj_bias_sb", [TILE, HID])
        gate_w_sb = sb("gate_w_sb", [HALF, 2, EXPERTS])
        attn_w_sb = sb("attn_w_sb", [HALF, 2, 2, 4 * HID], F32R)

        x_sb = two("x_sb", [128, KP, PAD])
        h_sb = sb("h_sb", [TILE, 2, HID])
        h_bias = two("h_bias", [TILE, 2, HID])
        xn = sb("xn", [TILE, 2, HID])
        stats = sb("stats", [TILE, 2, 6])
        mean_var = sb("mean_var", [TILE, 2, 2])
        var_eps = sb("var_eps", [TILE, 2])
        rstd = sb("rstd", [TILE, 2])
        xt_hi = sb("xt_hi", [HALF, 2, PAD], F32R)
        xt_lo = sb("xt_lo", [HALF, 2, PAD], F32R)
        k_hi = sb("k_hi", [HALF, 2, PAD], F32R)
        k_lo = sb("k_lo", [HALF, 2, PAD], F32R)
        q_hi = two("q_hi", [128, 2, PAD], F32R)
        q_lo = two("q_lo", [HALF, 2, PAD], F32R)
        km_hi = two("km_hi", [128, HEADS, PAD], F32R)
        km_lo = two("km_lo", [HALF, HEADS, PAD], F32R)
        v_sb = two("v_sb", [TILE, 2, HEADS, 32])
        row_max = sb("row_max", [TILE, 2, HEADS])
        neg_max = sb("neg_max", [TILE, 2 * HEADS], F32R)
        max_cols = sb("max_cols", [TILE, 4, 128])
        pt = sb("pt", [TILE, HEADS, PCOLS])
        ot = sb("ot", [128, GROUPS, PAD])
        sum_inv = sb("sum_inv", [TILE, 2, HEADS])
        o_tok = sb("o_tok", [TILE, 2, HID])
        o_hi = sb("o_hi", [HALF, 2, PAD], F32R)
        o_lo = sb("o_lo", [HALF, 2, PAD], F32R)
        h2 = two("h2", [TILE, 2, HID])
        stats2 = sb("stats2", [TILE, 2, 6])
        mean_var2 = sb("mean_var2", [TILE, 2, 2])
        var_eps2 = sb("var_eps2", [TILE, 2])
        rstd2 = sb("rstd2", [TILE, 2])
        xn2 = sb("xn2", [TILE, 2, HID])
        xt2_hi = two("xt2_hi", [HALF, 2, PAD], F32R)
        xt2_lo = two("xt2_lo", [HALF, 2, PAD], F32R)
        gate_sum = sb("gate_sum", [HALF, 2])
        logit = sb("logit", [1, EXPERTS])
        neg_top = sb("neg_top", [1, 1])
        gate_exp = sb("gate_exp", [1, EXPERTS])
        gate_den = sb("gate_den", [1, 1])
        gate_prob = sb("gate_prob", [1, 1])
        below_top = sb("below_top", [1, EXPERTS])
        second = sb("second", [1, 1])
        choice = sb("choice", [1, 1], I32)
        weight = two("weight", [TILE, 1])
        w1_sb = two("w1_sb", [HALF, 2, 2, FFN], F32R)
        w2_sb = two("w2_sb", [128, W2COLS])
        b2_sb = two("b2_sb", [TILE, HID])
        act_sb = sb("act_sb", [128, FCH, PAD])
        y_sb = sb("y_sb", [TILE, 2, HID])
        out_sb = two("out_sb", [TILE, 2, HID])

        score = [ctx.enter_context(nc.psum_tensor(f"score{i}", [128, 2, 512], F32)) for i in range(2)]
        dense = [ctx.enter_context(nc.psum_tensor(f"dense{i}", [128, 512], F32)) for i in range(2)]
        turned = ctx.enter_context(nc.psum_tensor("turned", [128, 512], F32))
        mixed = ctx.enter_context(nc.psum_tensor("mixed", [128, 512], F32))

        s_small = sem("s_small")
        s_big = [sem(f"s_big{i}") for i in range(2)]
        s_zero = sem("s_zero")
        s_const = sem("s_const")
        s_split = sem("s_split")
        s_saved = [sem(f"s_saved{i}") for i in range(2)]
        x_in = [sem(f"x_in{i}") for i in range(2)]
        patch_mm = sem("patch_mm")
        h_ready = sem("h_ready")
        var_ready = sem("var_ready")
        rstd_ready = sem("rstd_ready")
        xn_ready = sem("xn_ready")
        hb_ready = sem("hb_ready")
        xt_mm = sem("xt_mm")
        xt_hi_ready = sem("xt_hi_ready")
        xt_lo_ready = sem("xt_lo_ready")
        qk_mm = sem("qk_mm")
        qk_hi_ready = sem("qk_hi_ready")
        qk_lo_ready = sem("qk_lo_ready")
        km_ready = sem("km_ready")
        v_mm = sem("v_mm")
        v_ready = sem("v_ready")
        smax_mm = sem("smax_mm")
        smax_done = sem("smax_done")
        negmax_ready = sem("negmax_ready")
        max_cols_ready = sem("max_cols_ready")
        max_mm = sem("max_mm")
        max_ready = sem("max_ready")
        score_mm = sem("score_mm")
        exp_done = sem("exp_done")
        causal_done = sem("causal_done")
        pv_mm = sem("pv_mm")
        ot_ready = sem("ot_ready")
        otr_mm = sem("otr_mm")
        inv_ready = sem("inv_ready")
        o_ready = sem("o_ready")
        o2_mm = sem("o2_mm")
        o_hi_ready = sem("o_hi_ready")
        o_lo_ready = sem("o_lo_ready")
        proj_mm = sem("proj_mm")
        h2_ready = sem("h2_ready")
        var2_ready = sem("var2_ready")
        rstd2_ready = sem("rstd2_ready")
        xn2_ready = sem("xn2_ready")
        xt2_mm = sem("xt2_mm")
        xt2_hi_ready = sem("xt2_hi_ready")
        xt2_lo_ready = sem("xt2_lo_ready")
        gsum_mm = sem("gsum_mm")
        gsum_ready = sem("gsum_ready")
        logit_mm = sem("logit_mm")
        logit_ready = sem("logit_ready")
        top_ready = sem("top_ready")
        gexp_done = sem("gexp_done")
        prob_ready = sem("prob_ready")
        choice_ready = sem("choice_ready")
        choice_read = sem("choice_read")
        weight_mm = sem("weight_mm")
        weight_ready = sem("weight_ready")
        w_in = [sem(f"w_in{i}") for i in range(2)]
        up_mm = sem("up_mm")
        gelu_done = sem("gelu_done")
        down_mm = sem("down_mm")
        y_ready = sem("y_ready")
        out_ready = sem("out_ready")
        stored = [sem(f"stored{i}") for i in range(2)]
        dve_step = sem("dve_step")
        unused = sem("unused")

        def score_slot(image, k):
            return (11 * image.par + k) % 2

        stage = pt[:, :, :].rearrange("p h c -> p (h c)")

        def staged(i):
            return stage[0:HALF, i * 2 * FFN:(i + 1) * 2 * FFN].rearrange("p (c n) -> p c n", c=2)

        def stand_alone(engine):
            engine.sem_inc(unused, 1)

        block = ctx.enter_context(nc.Block())

        @block.sync
        def _(sp):
            sp.dma_start(staged(0), attn_w.rearrange("(c p) n -> p c n", c=2)).then_inc(s_big[0], 16)
            sp.dma_start(x_sb[0][:], x[0]).then_inc(x_in[0], 16)
            sp.dma_start(tok_w_sb[:], tok_w).then_inc(s_small, 16)
            sp.dma_start(tok_bias_sb[:, 0, :], tok_bias.partition_broadcast(TILE)).then_inc(s_small, 16)
            sp.dma_start(tok_bias_sb[:, 1, :], tok_bias.partition_broadcast(TILE)).then_inc(s_small, 16)
            sp.dma_start(proj_bias_sb[:], proj_bias.partition_broadcast(TILE)).then_inc(s_small, 16)
            sp.dma_start(gate_w_sb[:], gate_w[1]).then_inc(s_small, 16)
            sp.wait_ge(s_small, 80)
            sp.dma_start(tok_bias_sb[0:1, 0, :], gate_w[0]).then_inc(s_small, 16)
            sp.dma_start(x_sb[1][:], x[1]).then_inc(x_in[1], 16)
            for e in range(EXPERTS):
                i = (e + 1) % 2
                if e >= 1:
                    sp.wait_ge(s_split, 2 * e)
                sp.dma_start(staged(i), w1[e].rearrange("(c p) n -> p c n", c=2)).then_inc(s_big[i], 16)
            for e in range(EXPERTS):
                sp.wait_ge(s_split, 2 * (e + 2))
                sp.dma_start(w1_split[e], w1_sb[e % 2][:].bitcast(F32).rearrange("p c s n -> p (c s n)")).then_inc(s_saved[e % 2], 16)
            sp.wait_ge(s_saved[0], 32)
            sp.wait_ge(s_saved[1], 16)

            def load_x(a):
                sp.wait_ge(patch_mm, a.back(2).count(2, 2))
                sp.dma_start(x_sb[a.par][:], x[a.index()]).then_inc(x_in[a.par], 16)

            def load_expert(c):
                sp.wait_ge(choice_ready, c.count(1, 1))
                stand_alone(sp)
                e = sp.value_load(choice[0:1, 0:1], min_val=0, max_val=EXPERTS - 1)
                if c.trip is not None or c.first >= 2:
                    sp.wait_ge(out_ready, c.back(2).count(2, 2))
                sp.dma_start(w1_sb[c.par][:].bitcast(F32).rearrange("p c s n -> p (c s n)"), w1_split[e]).then_inc(w_in[c.par], 16)
                sp.dma_start(w2_sb[c.par][:], w2b1[e]).then_inc(w_in[c.par], 16)
                sp.dma_start(b2_sb[c.par][:], b2[e].partition_broadcast(TILE)).then_inc(w_in[c.par], 16)
                sp.sem_inc(choice_read, 1)

            def store(d):
                for j in range(2):
                    sp.wait_ge(out_ready, d.count(2, j + 1))
                    rows = TILE - j
                    sp.dma_start(out[d.index(), j * TILE:j * TILE + rows, :],
                                 out_sb[d.par][0:rows, j, :]).then_inc(stored[d.par], 16)

            def turn(n, trip):
                a, c, d = (Image(n + k, trip) for k in (2, -1, -2))
                if c.real():
                    load_expert(c)
                if d.real():
                    store(d)
                if a.real() and n >= 0:
                    load_x(a)

            run_turns(sp, turn)
            for s in stored:
                sp.wait_ge(s, 16 * IMAGES)

        @block.gpsimd
        def _(pool):
            g = nc.gpsimd
            g.memset(ident[:], 0.0).then_inc(s_zero, 1)
            g.memset(ident_b[:], 0.0).then_inc(s_zero, 1)
            g.memset(causal0[:], 0.0).then_inc(s_zero, 1)
            g.memset(causal1[:], 0.0).then_inc(s_zero, 1)
            g.memset(head_rows[:], 1.0).then_inc(s_zero, 1)
            g.memset(pick_max[:], 0.0).then_inc(s_zero, 1)
            g.memset(real_tok[:], 1.0).then_inc(s_zero, 1)
            g.memset(ones_row[:], 1.0).then_inc(s_const, 1)
            g.memset(minus_half[:], -0.5).then_inc(s_const, 1)
            g.memset(max_cols[:], 0.0).then_inc(s_const, 1)
            for i in range(2):
                g.memset(v_sb[i][:], 0.0).then_inc(s_zero, 1)
            pool.wait_ge(s_zero, 9)
            g.affine_select(out=ident[:], in_=ident[:], compare_op=ALU.not_equal, fill=1.0, base=0,
                            pattern=[[-1, 128]], channel_multiplier=1).then_inc(s_const, 1)
            g.affine_select(out=ident_b[:], in_=ident_b[:], compare_op=ALU.not_equal, fill=1.0, base=0,
                            pattern=[[-1, TILE]], channel_multiplier=1).then_inc(s_const, 1)
            g.affine_select(out=causal0[:], in_=causal0[:], compare_op=ALU.is_ge, fill=BIG, base=0,
                            pattern=[[-1, KEYS0]], channel_multiplier=1).then_inc(s_const, 1)
            g.affine_select(out=causal1[:], in_=causal1[:], compare_op=ALU.is_ge, fill=BIG, base=1,
                            pattern=[[-1, KEYS0]], channel_multiplier=1).then_inc(s_const, 1)
            g.affine_select(out=real_tok[:], in_=real_tok[:], compare_op=ALU.not_equal, fill=0.0,
                            base=-(TILE - 1 + 1), pattern=[[1, 2]], channel_multiplier=1).then_inc(s_const, 1)
            g.affine_select(out=head_rows[:], in_=head_rows[:], compare_op=ALU.is_ge, fill=0.0, base=0,
                            pattern=[[-HD, HPC]], channel_multiplier=1).then_inc(s_zero, 1)
            pool.wait_ge(s_zero, 10)
            g.affine_select(out=head_rows[:], in_=head_rows[:], compare_op=ALU.is_ge, fill=0.0, base=HD - 1,
                            pattern=[[HD, HPC]], channel_multiplier=-1).then_inc(s_const, 1)
            for part in range(2):
                g.affine_select(out=pick_max[:], in_=pick_max[:], compare_op=ALU.not_equal,
                                fill=1.0, base=-MROW - HPC * part, pattern=[[-1, HPC]],
                                channel_multiplier=1).then_inc(s_zero, 1)
                pool.wait_ge(s_zero, 11 + part)
            for i in range(2):
                g.memset(v_sb[i][:, :, :, HD:HD + 1], 1.0).then_inc(s_const, 1)

            def rstd_of(image, ready, src, done, dst):
                pool.wait_ge(ready, image.count(1, 1))
                g.tensor_tensor(dst[:], src[:], minus_half[:], ALU.pow).then_inc(done, 1)

            def residual_bias(a):
                pool.wait_ge(h_ready, a.count(2, 2))
                if a.trip is not None or a.first >= 2:
                    pool.wait_ge(h2_ready, a.back(2).count(2, 2))
                g.tensor_tensor(h_bias[a.par][:], h_sb[:],
                                proj_bias_sb[:].unsqueeze(1).to_broadcast([TILE, 2, HID]), ALU.add).then_inc(hb_ready, 1)

            def split_heads(a, c, part, first=0, last=HPC):
                src, dst = ((k_hi, km_hi), (k_lo, km_lo))[part]
                if first == 0:
                    pool.wait_ge((qk_hi_ready, qk_lo_ready)[part], a.count(4, c + 1))
                    if c == 0 and part == 0 and (a.trip is not None or a.first >= 2):
                        pool.wait_ge(score_mm, a.back(2).count(6, 6))
                stand_alone(pool)
                for h in range(first, last):
                    g.tensor_scalar(dst[a.par][0:HALF, c * HPC + h, :], src[:, c, :].bitcast(F32),
                                    head_rows[:, h:h + 1], 1.0, ALU.mult, ALU.mult).then_inc(km_ready, 1)

            def hide_future(b, s):
                pool.wait_ge(exp_done, b.count(6, s + 1))
                stand_alone(pool)
                v = pt[:, 2 * s:2 * s + 2, 0:2 * KEYS0].rearrange("p h (r q) -> p h r q", r=2)
                g.affine_select(out=v, in_=v, compare_op=ALU.is_ge, fill=0.0, base=-1,
                                pattern=[[0, 2], [1, 2], [1, KEYS0]], channel_multiplier=-1).then_inc(causal_done, 1)

            pool.wait_ge(s_small, 96)
            pool.wait_ge(s_const, 11)

            def turn(n, trip):
                a, b, c = (Image(n + k, trip) for k in (1, 0, -1))
                if a.real():
                    rstd_of(a, var_ready, var_eps, rstd_ready, rstd)
                if c.real():
                    rstd_of(c, var2_ready, var_eps2, rstd2_ready, rstd2)
                if a.real():
                    residual_bias(a)
                for s in range(6):
                    if b.real():
                        hide_future(b, s)
                    if a.real():
                        if s == 1:
                            split_heads(a, 0, 0)
                        elif s == 2:
                            split_heads(a, 0, 1)
                        elif s == 3:
                            split_heads(a, 1, 0)
                        elif s == 5:
                            split_heads(a, 1, 1)

            run_turns(pool, turn)

        @block.scalar
        def _(act):
            act.wait_ge(s_zero, 12)
            for i in range(2):
                for c in range(2):
                    nc.scalar.activation(km_hi[i][MROW:128, c * HPC:(c + 1) * HPC, :],
                                         pick_max[MROW:128, :].unsqueeze(2).to_broadcast([128 - MROW, HPC, PAD]),
                                         ACT.Copy).then_inc(s_const, 1)

            def hi(image, dst, src, ready, per, k, done):
                act.wait_ge(ready, image.count(per, k))
                nc.scalar.activation(dst, src, ACT.Copy).then_inc(done, 1)

            def both(bank):
                return bank[0:HALF, 0:2 * PAD].rearrange("p (c t) -> p c t", c=2)

            def xt(a):
                if a.trip is not None or a.first >= 1:
                    act.wait_ge(v_mm, a.back(1).count(2, 2))
                hi(a, xt_hi[:], both(turned), xt_mm, 1, 1, xt_hi_ready)

            def qk(a, u):
                dst = k_hi[:, u, :] if u < 2 else q_hi[a.par][0:HALF, u - 2, :]
                if u == 0 and (a.trip is not None or a.first >= 1):
                    act.wait_ge(km_ready, a.back(1).count(2 * HEADS, 2 * HEADS))
                hi(a, dst, dense[u % 2][0:HALF, 0:PAD], qk_mm, 4, u + 1, qk_hi_ready)

            def values(a, t):
                act.wait_ge(v_mm, a.count(2, t + 1))
                if t == 0 and (a.trip is not None or a.first >= 2):
                    act.wait_ge(pv_mm, a.back(2).count(GROUPS, GROUPS))
                nc.scalar.activation(v_sb[a.par][:, t, :, 0:HD],
                                     dense[t][0:TILE, 0:HID].rearrange("p (h d) -> p h d", h=HEADS),
                                     ACT.Copy).then_inc(v_ready, 1)

            def max_rows(b):
                act.wait_ge(max_mm, b.count(1, 1))
                nc.scalar.activation(q_hi[b.par][MROW:128, :, :],
                                     mixed[MROW:128, 0:2 * PAD].rearrange("p (c t) -> p c t", c=2),
                                     ACT.Copy).then_inc(max_ready, 1)

            def exps(b, s):
                act.wait_ge(score_mm, b.count(6, s + 1))
                if s % 2 == 0 and (b.trip is not None or b.first >= 1):
                    act.wait_ge(pv_mm, b.back(1).count(GROUPS, s // 2 + 1))
                nc.scalar.activation(pt[:, 2 * s:2 * s + 2, :],
                                     score[score_slot(b, 5 + s)][0:TILE, :, 2 * PAD - PCOLS:2 * PAD],
                                     ACT.Exp, scale=HD ** -0.5).then_inc(exp_done, 1)

            def mixed_out(b, g):
                act.wait_ge(pv_mm, b.count(GROUPS, g + 1))
                if g == 0 and (b.trip is not None or b.first >= 1):
                    act.wait_ge(otr_mm, b.back(1).count(2, 2))
                nc.scalar.activation(ot[:, g, :], mixed[:, 0:PAD], ACT.Copy).then_inc(ot_ready, 1)

            def o_high(c):
                if c.trip is not None or c.first >= 1:
                    act.wait_ge(proj_mm, c.back(1).count(2, 2))
                hi(c, o_hi[:], both(mixed), o2_mm, 1, 1, o_hi_ready)

            def xt2(c):
                if c.trip is not None or c.first >= 2:
                    act.wait_ge(up_mm, c.back(2).count(FCH, FCH))
                hi(c, xt2_hi[c.par][:], both(mixed), xt2_mm, 1, 1, xt2_hi_ready)

            def gate_exps(c):
                act.wait_ge(top_ready, c.count(1, 1))
                nc.scalar.activation(gate_exp[:], logit[:], ACT.Exp, bias=neg_top[:],
                                     accum_out=gate_den[:]).then_inc(gexp_done, 1)

            def gelu(d, m):
                act.wait_ge(up_mm, d.count(FCH, m + 1))
                if m == 0 and (d.trip is not None or d.first >= 1):
                    act.wait_ge(down_mm, d.back(1).count(2, 2))
                nc.scalar.activation(act_sb[:, m, :], dense[m % 2][:, 0:PAD], ACT.Gelu,
                                     bias=w2_sb[d.par][:, FCH * HID + m:FCH * HID + m + 1]).then_inc(gelu_done, 1)

            def turn(n, trip):
                a, b, c, d = (Image(n + k, trip) for k in (1, 0, -1, -2))
                A, B, C, D = a.real(), b.real(), c.real(), d.real()
                if C:
                    o_high(c)
                if A:
                    xt(a)
                if D:
                    gelu(d, 0), gelu(d, 1), gelu(d, 2)
                if B:
                    max_rows(b)
                if D:
                    gelu(d, 3), gelu(d, 4), gelu(d, 5)
                if C:
                    xt2(c)
                if B:
                    exps(b, 0)
                if A:
                    qk(a, 0)
                if C:
                    gate_exps(c)
                if B:
                    exps(b, 1)
                if A:
                    qk(a, 1)
                if B:
                    mixed_out(b, 0)
                    exps(b, 2)
                if A:
                    qk(a, 2)
                if B:
                    exps(b, 3)
                if A:
                    qk(a, 3)
                if B:
                    mixed_out(b, 1)
                    exps(b, 4)
                if A:
                    values(a, 0)
                if B:
                    exps(b, 5)
                if A:
                    values(a, 1)
                if B:
                    mixed_out(b, 2)

            run_turns(act, turn)

        @block.vector
        def _(dve):
            v = nc.vector
            for i in range(EXPERTS + 1):
                half = i % 2
                dve.wait_ge(s_big[half], 16 * (i // 2 + 1))
                dst = attn_w_sb if i == 0 else w1_sb[(i - 1) % 2]
                if i == EXPERTS:
                    dve.wait_ge(s_saved[0], 16)
                v.tensor_copy(dst[:, :, 0, :], staged(half)).then_inc(s_split, 1)
                dve.wait_ge(s_split, 2 * i + 1)
                v.tensor_tensor(dst[:, :, 1, :], staged(half), dst[:, :, 0, :].bitcast(F32),
                                ALU.subtract).then_inc(s_split, 1)
            dve.wait_ge(s_const, 15)
            dve.wait_ge(s_small, 96)

            def low(image, dst, src, high, ready, per, k, done):
                dve.wait_ge(ready, image.count(per, k))
                v.tensor_tensor(dst, src, high.bitcast(F32), ALU.subtract).then_inc(done, 1)

            def both(bank):
                return bank[0:HALF, 0:2 * PAD].rearrange("p (c t) -> p c t", c=2)

            class Steps:
                per_turn = 12

                def __init__(self):
                    self.n, self.trip = 0, None

                def link(self, instruction):
                    instruction.then_inc(dve_step, 1)
                    self.n += 1
                    dve.wait_ge(dve_step, self.n if self.trip is None else self.trip * (2 * self.per_turn) + self.n)

            steps = Steps()
            link = steps.link

            def block_max(b, k):
                dve.wait_ge(smax_mm, b.count(5, k + 1))
                if k == 0 and (b.trip is not None or b.first >= 1):
                    dve.wait_ge(max_cols_ready, b.back(1).count(1, 1))
                slot = score[score_slot(b, k)]
                if k < 2:
                    v.reduce_max(row_max[:, 0, k * HPC:(k + 1) * HPC].rearrange("p (z h) -> p z h", z=2),
                                 slot[0:TILE, :, 0:3 * KEYS0].rearrange("p z (h k) -> p z h k", h=3),
                                 AX_X).then_inc(smax_done, 1)
                else:
                    h = 4 * (k - 2)
                    v.reduce_max(row_max[:, 1, h:h + 4].rearrange("p (z h) -> p z h", z=2),
                                 slot[0:TILE, :, 0:2 * PAD].rearrange("p z (h k) -> p z h k", h=2),
                                 AX_X).then_inc(smax_done, 1)

            def normalise(c, j):
                bank = (mixed, turned)[j]
                view = bank[0:TILE, 0:HEADS * 32].rearrange("p (h e) -> p h e", h=HEADS)
                dve.wait_ge(otr_mm, c.count(2, j + 1))
                if j == 0 and (c.trip is not None or c.first >= 1):
                    dve.wait_ge(o2_mm, c.back(1).count(1, 1))
                v.reciprocal(sum_inv[:, j, :], view[:, :, HD]).then_inc(inv_ready, 1)
                dve.wait_ge(inv_ready, c.count(2, j + 1))
                v.tensor_tensor(o_tok[:, j, :].rearrange("p (h e) -> p h e", h=HEADS), view[:, :, 0:HD],
                                sum_inv[:, j, :].unsqueeze(2).to_broadcast([TILE, HEADS, HD]),
                                ALU.mult).then_inc(o_ready, 1)

            def embed(a, t):
                dve.wait_ge(patch_mm, a.count(2, t + 1))
                if t == 0 and (a.trip is not None or a.first >= 1):
                    dve.wait_ge(hb_ready, a.back(1).count(1, 1))
                v.tensor_tensor(h_sb[:, t, :], dense[t][0:TILE, 0:HID], tok_bias_sb[:, t, :], ALU.add).then_inc(h_ready, 1)
                dve.wait_ge(h_ready, a.count(2, t + 1))
                link(v.bn_stats(stats[:, t, :], h_sb[:, t, :]))
                stand_alone(dve)
                link(v.bn_aggr(mean_var[:, t, :], stats[:, t, :]))

            def residual(c, j):
                dve.wait_ge(proj_mm, c.count(2, j + 1))
                if j == 0:
                    dve.wait_ge(hb_ready, c.count(1, 1))
                v.tensor_tensor(h2[c.par][:, j, :], dense[j][0:TILE, 0:HID], h_bias[c.par][:, j, :],
                                ALU.add).then_inc(h2_ready, 1)
                dve.wait_ge(h2_ready, c.count(2, j + 1))
                link(v.bn_stats(stats2[:, j, :], h2[c.par][:, j, :]))
                stand_alone(dve)
                link(v.bn_aggr(mean_var2[:, j, :], stats2[:, j, :]))

            def variance(dst, mv, done):
                v.tensor_scalar(dst[:], mv[:, :, 1], EPS, None, ALU.add).then_inc(done, 1)

            def layer_norm(image, dst, src, mv, rs, ready, done, used):
                dve.wait_ge(ready, image.count(1, 1))
                if image.trip is not None or image.first >= 1:
                    sem_used, per = used
                    dve.wait_ge(sem_used, image.back(1).count(per, per))
                for t in range(2):
                    v.tensor_scalar(dst[:, t, :], src[:, t, :], mv[:, t, 0:1], rs[:, t:t + 1],
                                    ALU.subtract, ALU.mult).then_inc(done, 1)

            def spread_max(b):
                m = row_max[:].rearrange("p j h -> p (j h)")
                dve.wait_ge(smax_done, b.count(5, 5))
                if b.trip is not None or b.first >= 1:
                    dve.wait_ge(max_mm, b.back(1).count(1, 1))
                v.tensor_scalar(neg_max[:], m, -1.0, None, ALU.mult).then_inc(negmax_ready, 1)
                dve.wait_ge(negmax_ready, b.count(1, 1))
                grouped = "p (g h) -> p g h"
                link(v.tensor_copy(max_cols[:, :, MROW:MROW + HPC],
                                   neg_max[:].bitcast(F32).rearrange(grouped, g=4)))
                v.scalar_tensor_tensor(out=max_cols[:, :, MROW + HPC:MROW + 2 * HPC],
                                       in0=m.rearrange(grouped, g=4), scalar=-1.0,
                                       in1=neg_max[:].bitcast(F32).rearrange(grouped, g=4),
                                       op0=ALU.mult, op1=ALU.subtract).then_inc(max_cols_ready, 1)

            def gate_sums(c):
                dve.wait_ge(gsum_mm, c.count(1, 1))
                v.tensor_copy(gate_sum[:], turned[0:HALF, 0:2]).then_inc(gsum_ready, 1)

            def gate(c):
                dve.wait_ge(logit_mm, c.count(1, 1))
                if c.trip is not None or c.first >= 1:
                    dve.wait_ge(gexp_done, c.back(1).count(1, 1))
                v.tensor_scalar(logit[:], turned[0:1, 0:EXPERTS], 1.0 / TOKENS, None, ALU.mult).then_inc(logit_ready, 1)
                dve.wait_ge(logit_ready, c.count(1, 1))
                link(v.reduce_max(second[:], logit[:], AX_X))
                v.tensor_scalar(neg_top[:], second[:], -1.0, None, ALU.mult).then_inc(top_ready, 1)
                link(v.tensor_scalar(below_top[:], logit[:], second[:], None, ALU.is_lt))
                link(v.tensor_scalar(second[:], below_top[:, 1:2], 1.0, None, ALU.add))
                if c.trip is not None or c.first >= 1:
                    dve.wait_ge(choice_read, c.back(1).count(1, 1))
                v.tensor_tensor(choice[:], second[:], below_top[:, 0:1], ALU.mult).then_inc(choice_ready, 1)

            def gate_weight(c):
                dve.wait_ge(gexp_done, c.count(1, 1))
                v.reciprocal(gate_prob[:], gate_den[:]).then_inc(prob_ready, 1)

            def spread_weight(c):
                dve.wait_ge(weight_mm, c.count(1, 1))
                v.tensor_copy(weight[c.par][:], turned[0:TILE, 0:1]).then_inc(weight_ready, 1)

            def finish(d, j):
                dve.wait_ge(down_mm, d.count(2, j + 1))
                if j == 0:
                    dve.wait_ge(w_in[d.par], d.turns(48, 48))
                    dve.wait_ge(weight_ready, d.count(1, 1))
                    if d.trip is not None or d.first >= 1:
                        dve.wait_ge(out_ready, d.back(1).count(2, 2))
                    if d.trip is not None or d.first >= 2:
                        dve.wait_ge(stored[d.par], d.turns(32, 0))
                v.tensor_tensor(y_sb[:, j, :], dense[j][0:TILE, 0:HID], b2_sb[d.par][:], ALU.add).then_inc(y_ready, 1)
                dve.wait_ge(y_ready, d.count(2, j + 1))
                v.scalar_tensor_tensor(out=out_sb[d.par][:, j, :], in0=y_sb[:, j, :], scalar=weight[d.par][:, 0:1],
                                       in1=h2[d.par][:, j, :], op0=ALU.mult, op1=ALU.add).then_inc(out_ready, 1)

            def qk_low(a, u):
                dst = k_lo[:, u, :] if u < 2 else q_lo[a.par][:, u - 2, :]
                high = k_hi[:, u, :] if u < 2 else q_hi[a.par][0:HALF, u - 2, :]
                low(a, dst, dense[u % 2][0:HALF, 0:PAD], high, qk_hi_ready, 4, u + 1, qk_lo_ready)

            def turn(n, trip):
                a, b, c, d = (Image(n + k, trip) for k in (1, 0, -1, -2))
                A, B, C, D = a.real(), b.real(), c.real(), d.real()
                if B:
                    block_max(b, 0), block_max(b, 1)
                if C:
                    normalise(c, 0), normalise(c, 1)
                if A:
                    embed(a, 0)
                if B:
                    block_max(b, 2)
                if C:
                    low(c, o_lo[:], both(mixed), o_hi[:], o_hi_ready, 1, 1, o_lo_ready)
                if A:
                    embed(a, 1)
                    variance(var_eps, mean_var, var_ready)
                if B:
                    block_max(b, 3)
                if C:
                    residual(c, 0), residual(c, 1)
                    variance(var_eps2, mean_var2, var2_ready)
                if B:
                    block_max(b, 4)
                if A:
                    layer_norm(a, xn, h_sb, mean_var, rstd, rstd_ready, xn_ready, (xt_mm, 1))
                if B:
                    spread_max(b)
                if A:
                    low(a, xt_lo[:], both(turned), xt_hi[:], xt_hi_ready, 1, 1, xt_lo_ready)
                if C:
                    layer_norm(c, xn2, h2[c.par], mean_var2, rstd2, rstd2_ready, xn2_ready, (gsum_mm, 1))
                    low(c, xt2_lo[c.par][:], both(mixed), xt2_hi[c.par][:], xt2_hi_ready, 1, 1, xt2_lo_ready)
                    gate_sums(c)
                if A:
                    qk_low(a, 0)
                if C:
                    gate(c)
                if A:
                    qk_low(a, 1)
                if C:
                    gate_weight(c)
                if A:
                    qk_low(a, 2)
                    qk_low(a, 3)
                if C:
                    spread_weight(c)
                if D:
                    finish(d, 0)
                    finish(d, 1)

            start = []

            def enter(trip):
                start.append(steps.n)
                steps.trip = trip

            def leave(trips):
                steps.trip = None
                assert steps.n - start[0] == 2 * steps.per_turn, (steps.n - start[0]) / 2
                steps.n += 2 * steps.per_turn * (trips - 1)

            run_turns(dve, turn, enter, leave)

        @block.tensor
        def _(pe):
            mm = nc.tensor.matmul
            turns = BankTurns(pe)
            pe.wait_ge(s_small, 96)
            pe.wait_ge(s_const, 15)
            pe.wait_ge(s_split, 2)

            def three(dst, pairs):
                ops = [p for lh, ll, rh, rl in pairs for p in ((lh, rh), (lh, rl), (ll, rh))]
                for i, (l, r) in enumerate(ops):
                    last = mm(dst, l, r, start=(i == 0), stop=(i == len(ops) - 1))
                return last

            def score_max(b, k):
                slot = score_slot(b, k)
                turns.take(("score", slot), b, smax_done, 5, k + 1)
                if k == 0:
                    pe.wait_ge(qk_hi_ready, b.count(4, 4))
                    pe.wait_ge(km_ready, b.count(2 * HEADS, 2 * HEADS))
                for z in range(2):
                    if k < 2:
                        h, heads, keys, t, hidden, first = k * HPC + 3 * z, 3, KEYS0, 0, causal0, 0
                    else:
                        h, heads, keys, t, hidden, first = 4 * (k - 2) + 2 * z, 2, PAD, 1, causal1, PAD - KEYS0
                    dst = score[slot][0:TILE, z, 0:heads * keys].rearrange("p (h k) -> p h k", h=heads)
                    mm(dst, q_hi[b.par][0:HALF, h // HPC, t * TILE:(t + 1) * TILE],
                       km_hi[b.par][0:HALF, h:h + heads, 0:keys], start=True, stop=False)
                    last = mm(dst[:, :, first:first + KEYS0], ident_b[:],
                              hidden[:].unsqueeze(1).to_broadcast([TILE, heads, KEYS0]), start=False, stop=True)
                last.then_inc(smax_mm, 1)

            def turn_max(b):
                turns.take("mixed", b, max_ready, 1, 1)
                pe.wait_ge(max_cols_ready, b.count(1, 1))
                for c in range(2):
                    for j in range(2):
                        last = nc.tensor.transpose(mixed[:, c * PAD + j * TILE:c * PAD + (j + 1) * TILE],
                                                   max_cols[:, 2 * j + c, :], ident[0:TILE, 0:TILE])
                last.then_inc(max_mm, 1)

            def scores(b, s):
                slot = score_slot(b, 5 + s)
                turns.take(("score", slot), b, exp_done, 6, s + 1)
                if s == 0:
                    pe.wait_ge(max_ready, b.count(1, 1))
                    pe.wait_ge(qk_lo_ready, b.count(4, 4))
                for z in range(2):
                    h = 2 * s + z
                    c = h // HPC
                    for i, t in enumerate((1, 0)):
                        dst = score[slot][0:TILE, z, i * PAD:(i + 1) * PAD]
                        keys = slice(t * TILE, (t + 1) * TILE)
                        mm(dst, km_hi[b.par][:, h, keys], q_hi[b.par][:, c, :], start=True, stop=False)
                        mm(dst, km_lo[b.par][:, h, keys], q_hi[b.par][0:HALF, c, :], start=False, stop=False)
                        last = mm(dst, km_hi[b.par][0:HALF, h, keys], q_lo[b.par][:, c, :], start=False, stop=True)
                last.then_inc(score_mm, 1)

            def mix(b, g):
                turns.take("mixed", b, ot_ready, GROUPS, g + 1)
                pe.wait_ge(causal_done, b.count(6, 2 * g + 2))
                if g == 0:
                    pe.wait_ge(v_ready, b.count(2, 2))
                for j in range(4):
                    h = 4 * g + j
                    mm(mixed[32 * j:32 * j + 32, 0:PAD], v_sb[b.par][:, 0, h, :], pt[:, h, KEYS0:PCOLS],
                       start=True, stop=False)
                    last = mm(mixed[32 * j:32 * j + 32, PAD - KEYS0:PAD], v_sb[b.par][:, 1, h, :],
                              pt[:, h, 0:KEYS0], start=False, stop=True)
                last.then_inc(pv_mm, 1)

            def turn_out(c, j):
                name, bank = (("mixed", mixed), ("turned", turned))[j]
                turns.take(name, c, o_ready, 2, j + 1)
                if j == 0:
                    pe.wait_ge(ot_ready, c.count(GROUPS, GROUPS))
                for g in range(GROUPS):
                    last = nc.tensor.transpose(bank[0:TILE, g * 128:(g + 1) * 128],
                                               ot[:, g, j * TILE:(j + 1) * TILE], ident[:])
                last.then_inc(otr_mm, 1)

            def turn_tokens(image, name, bank, src, ready, per, done, read_done):
                turns.take(name, image, read_done, 1, 1)
                pe.wait_ge(ready, image.count(per, per))
                for c in range(2):
                    for j in range(2):
                        last = nc.tensor.transpose(bank[0:HALF, c * PAD + j * TILE:c * PAD + (j + 1) * TILE],
                                                   src[:, j, c * HALF:(c + 1) * HALF], ident[0:TILE, 0:TILE])
                last.then_inc(done, 1)

            def patches(a, t):
                turns.take(f"dense{t}", a, h_ready, 2, t + 1)
                if t == 0:
                    pe.wait_ge(x_in[a.par], a.turns(16, 16))
                for k in range(KP):
                    last = mm(dense[t][0:TILE, 0:HID], x_sb[a.par][:, k, t * TILE:(t + 1) * TILE], tok_w_sb[:, k, :],
                              start=(k == 0), stop=(k == KP - 1))
                last.then_inc(patch_mm, 1)

            def weights(c, part, first, n):
                return attn_w_sb[:, c, part, first:first + n]

            def qk(a, u):
                turns.take(f"dense{u % 2}", a, qk_lo_ready, 4, u + 1)
                if u == 0:
                    pe.wait_ge(xt_lo_ready, a.count(1, 1))
                first = (HID if u < 2 else 0) + (u % 2) * HALF
                three(dense[u % 2][0:HALF, 0:PAD],
                      [(weights(c, 0, first, HALF), weights(c, 1, first, HALF), xt_hi[:, c, :], xt_lo[:, c, :])
                       for c in range(2)]).then_inc(qk_mm, 1)

            def values(a, t):
                turns.take(f"dense{t}", a, v_ready, 2, t + 1)
                tok = slice(t * TILE, (t + 1) * TILE)
                three(dense[t][0:TILE, 0:HID],
                      [(xt_hi[:, c, tok], xt_lo[:, c, tok], weights(c, 0, 2 * HID, HID), weights(c, 1, 2 * HID, HID))
                       for c in range(2)]).then_inc(v_mm, 1)

            def project(c, j):
                turns.take(f"dense{j}", c, h2_ready, 2, j + 1)
                if j == 0:
                    pe.wait_ge(o_lo_ready, c.count(1, 1))
                tok = slice(j * TILE, (j + 1) * TILE)
                three(dense[j][0:TILE, 0:HID],
                      [(o_hi[:, k, tok], o_lo[:, k, tok], weights(k, 0, 3 * HID, HID), weights(k, 1, 3 * HID, HID))
                       for k in range(2)]).then_inc(proj_mm, 1)

            def gate_sums(c):
                turns.take("turned", c, gsum_ready, 1, 1)
                for k in range(2):
                    for j in range(2):
                        last = mm(turned[0:HALF, k:k + 1], xn2[:, j, k * HALF:(k + 1) * HALF],
                                  real_tok[:, j:j + 1], start=(j == 0), stop=(j == 1))
                last.then_inc(gsum_mm, 1)

            def logits(c):
                pe.wait_ge(gsum_ready, c.count(1, 1))
                turns.take("turned", c, logit_ready, 1, 1)
                for k in range(2):
                    last = mm(turned[0:1, 0:EXPERTS], gate_sum[:, k:k + 1], gate_w_sb[:, k, :],
                              start=(k == 0), stop=(k == 1))
                last.then_inc(logit_mm, 1)

            def spread_weight(c):
                turns.take("turned", c, weight_ready, 1, 1)
                pe.wait_ge(prob_ready, c.count(1, 1))
                mm(turned[0:TILE, 0:1], ones_row[:], gate_prob[:], start=True, stop=True).then_inc(weight_mm, 1)

            def up(d, m):
                turns.take(f"dense{m % 2}", d, gelu_done, FCH, m + 1)
                if m == 0:
                    pe.wait_ge(w_in[d.par], d.turns(48, 48))
                    pe.wait_ge(xt2_lo_ready, d.count(1, 1))
                cols = slice(m * 128, (m + 1) * 128)
                three(dense[m % 2][:, 0:PAD],
                      [(w1_sb[d.par][:, k, 0, cols], w1_sb[d.par][:, k, 1, cols], xt2_hi[d.par][:, k, :],
                        xt2_lo[d.par][:, k, :]) for k in range(2)]).then_inc(up_mm, 1)

            def down(d, j):
                turns.take(f"dense{j}", d, y_ready, 2, j + 1)
                if j == 0:
                    pe.wait_ge(gelu_done, d.count(FCH, FCH))
                for m in range(FCH):
                    last = mm(dense[j][0:TILE, 0:HID], act_sb[:, m, j * TILE:(j + 1) * TILE],
                              w2_sb[d.par][:, m * HID:(m + 1) * HID], start=(m == 0), stop=(m == FCH - 1))
                last.then_inc(down_mm, 1)

            def turn(n, trip):
                a, b, c, d = (Image(n + k, trip) for k in (1, 0, -1, -2))
                A, B, C, D = a.real(), b.real(), c.real(), d.real()
                if B:
                    score_max(b, 0), score_max(b, 1)
                if C:
                    turn_out(c, 0), turn_out(c, 1)
                if A:
                    patches(a, 0)
                if B:
                    score_max(b, 2)
                if C:
                    turn_tokens(c, "mixed", mixed, o_tok, o_ready, 2, o2_mm, o_lo_ready)
                if A:
                    patches(a, 1)
                if B:
                    score_max(b, 3)
                if C:
                    project(c, 0), project(c, 1)
                if B:
                    score_max(b, 4)
                if A:
                    turn_tokens(a, "turned", turned, xn, xn_ready, 2, xt_mm, xt_lo_ready)
                if D:
                    up(d, 0), up(d, 1), up(d, 2)
                if B:
                    turn_max(b)
                if D:
                    up(d, 3), up(d, 4), up(d, 5)
                if C:
                    turn_tokens(c, "mixed", mixed, xn2, xn2_ready, 2, xt2_mm, xt2_lo_ready)
                    gate_sums(c)
                if B:
                    scores(b, 0)
                if A:
                    qk(a, 0)
                if C:
                    logits(c)
                if B:
                    scores(b, 1)
                if A:
                    qk(a, 1)
                if B:
                    mix(b, 0)
                    scores(b, 2)
                if A:
                    qk(a, 2)
                if B:
                    scores(b, 3)
                if A:
                    qk(a, 3)
                if C:
                    spread_weight(c)
                if B:
                    mix(b, 1)
                if D:
                    down(d, 0)
                if B:
                    scores(b, 4)
                if A:
                    values(a, 0)
                if B:
                    scores(b, 5)
                if A:
                    values(a, 1)
                if D:
                    down(d, 1)
                if B:
                    mix(b, 2)

            def enter(trip):
                turns.trip = trip

            run_turns(pe, turn, enter, turns.leave)


def kernel(x, cls_tok, L0_tok_W_proj, L0_tok_b_proj, L0_attn_w_attn, L0_attn_w_proj, L0_attn_b_proj,
           L0_ffn_Wg, L0_ffn_W1, L0_ffn_b1, L0_ffn_W2, L0_ffn_b2):
    import numpy as np
    import concourse.bacc as bacc
    from concourse.bass_utils import run_bass_kernel_spmd

    cut = np.asarray(x).reshape(IMAGES, GRID, PATCH, GRID, PATCH, CH).transpose(0, 2, 4, 5, 1, 3)
    cols = np.zeros((IMAGES, 128, KP, PAD), np.float32)
    cols[:, :, :, 1:TOKENS] = cut.reshape(IMAGES, 128, KP, GRID * GRID)
    arrays = {
        "x_cols": cols,
        "tok_w": np.ascontiguousarray(np.asarray(L0_tok_W_proj).reshape(128, KP, HID)),
        "tok_bias": np.asarray(L0_tok_b_proj),
        "attn_w": np.concatenate([np.asarray(L0_attn_w_attn), np.asarray(L0_attn_w_proj)], axis=1),
        "proj_bias": np.asarray(L0_attn_b_proj),
        "cls": np.asarray(cls_tok).reshape(1, HID),
        "gate_w": np.ascontiguousarray(np.asarray(L0_ffn_Wg).reshape(EXPERTS, 2, HALF).transpose(2, 1, 0)),
        "w1": np.asarray(L0_ffn_W1),
        "w2b1": np.concatenate([
            np.asarray(L0_ffn_W2).reshape(EXPERTS, FCH, 128, HID).transpose(0, 2, 1, 3).reshape(EXPERTS, 128, FCH * HID),
            np.asarray(L0_ffn_b1).reshape(EXPERTS, FCH, 128).transpose(0, 2, 1)], axis=2),
        "b2": np.asarray(L0_ffn_b2),
    }
    nc = bacc.Bacc("TRN2", target_bir_lowering=False, num_devices=1)
    aps = {k: nc.dram_tensor(k, v.shape, F32, kind="ExternalInput").ap() for k, v in arrays.items()}
    out = nc.dram_tensor("out", (IMAGES, TOKENS, HID), F32, kind="ExternalOutput").ap()
    vit_tower(nc, aps["x_cols"], aps["tok_w"], aps["tok_bias"], aps["attn_w"], aps["proj_bias"],
              (aps["cls"], aps["gate_w"]), aps["w1"], aps["w2b1"], aps["b2"], out)
    result = run_bass_kernel_spmd(nc, [arrays], core_ids=[0])
    return result.results[0]["out"]
```

```python
import concourse.bass as bass
from concourse import mybir
from contextlib import ExitStack

F32 = mybir.dt.float32
F32R = mybir.dt.float32r
BF16 = mybir.dt.bfloat16
I32 = mybir.dt.int32
ALU = mybir.AluOpType
ACT = mybir.ActivationFunctionType
AX_X = mybir.AxisListType.X

IMAGES, GRID, PATCH, CH = 64, 14, 16, 3
HID, HEADS, EXPERTS, FFN = 192, 12, 3, 768
HD = HID // HEADS
TOKENS = GRID * GRID + 1
PAD = TOKENS + 1
TILE = PAD // 2
PD = PATCH * PATCH * CH
KP = PD // 128
HALF = HID // 2
HPC = HEADS // 2
PPC = HPC // 2
STACK_DMAS = 3 * PPC * 3
FCH = FFN // 128
GROUPS = HEADS // 4
KEYS0 = TILE + 1
PCOLS = PAD + KEYS0
MROW = 96
EPS = 1e-5
BIG = -1e30
W2COLS = FCH * HID + FCH


class Image:

    def __init__(self, first, trip=None):
        self.first, self.trip = first, trip
        self.par = first % 2

    def count(self, per, more):
        c = per * self.first + more
        return c if self.trip is None else self.trip * (2 * per) + c

    def turns(self, per, more):
        c = per * (self.first // 2) + more
        return c if self.trip is None else self.trip * per + c

    def back(self, k):
        return Image(self.first - k, self.trip)

    def real(self):
        return self.trip is not None or 0 <= self.first < IMAGES

    def index(self):
        return self.first if self.trip is None else self.trip * 2 + self.first


class BankTurns:

    def __init__(self, pe):
        self.pe, self.last, self.trip = pe, {}, None

    def take(self, bank, image, read_done, per, more):
        if bank in self.last:
            sem, p, m, first = self.last[bank]
            self.pe.wait_ge(sem, Image(first, self.trip).count(p, m))
        self.last[bank] = (read_done, per, more, image.first)

    def leave(self, trips):
        self.last = {b: (s, p, m, f + 2 * (trips - 1)) for b, (s, p, m, f) in self.last.items()}
        self.trip = None


def run_turns(engine, turn, enter=None, leave=None):
    for n in range(-1, 3):
        turn(n, None)
    trips = (IMAGES - 6) // 2
    with engine.Fori(0, trips) as trip:
        if enter:
            enter(trip)
        turn(3, trip)
        turn(4, trip)
    if leave:
        leave(trips)
    for n in range(3 + 2 * trips, IMAGES + 2):
        turn(n, None)


def vit_tower(nc, x, tok_w, tok_bias, attn_w, proj_bias, gate_w, w1, w2b1, b2, out):
    ctx = ExitStack()
    with ctx:
        def sb(name, shape, dt=F32):
            return ctx.enter_context(nc.sbuf_tensor(name, shape, dt))

        def two(name, shape, dt=F32):
            return [sb(f"{name}{i}", shape, dt) for i in range(2)]

        def sem(name):
            return ctx.enter_context(nc.semaphore(name))

        w1_split = nc.dram_tensor("w1_split", [EXPERTS, HALF, 4 * FFN], F32, kind="Internal").ap()

        ident = sb("ident", [128, 128])
        ident_b = sb("ident_b", [TILE, TILE], BF16)
        causal0 = sb("causal0", [TILE, KEYS0], BF16)
        causal1 = sb("causal1", [TILE, KEYS0], BF16)
        pick_max = sb("pick_max", [128, HPC])
        real_tok = sb("real_tok", [TILE, 2])
        ones_row = sb("ones_row", [1, TILE])
        minus_half = sb("minus_half", [TILE, 2])
        tok_w_sb = sb("tok_w_sb", [128, KP, HID])
        tok_bias_sb = sb("tok_bias_sb", [TILE, 2, HID])
        proj_bias_sb = sb("proj_bias_sb", [TILE, HID])
        gate_w_sb = sb("gate_w_sb", [HALF, 2, EXPERTS])
        attn_w_sb = sb("attn_w_sb", [HALF, 2, 2, 4 * HID], F32R)

        x_sb = two("x_sb", [128, KP, PAD])
        h_sb = sb("h_sb", [TILE, 2, HID])
        h_bias = two("h_bias", [TILE, 2, HID])
        xn = sb("xn", [TILE, 2, HID])
        stats = sb("stats", [TILE, 2, 6])
        mean_var = sb("mean_var", [TILE, 2, 2])
        var_eps = sb("var_eps", [TILE, 2])
        rstd = sb("rstd", [TILE, 2])
        xt_hi = sb("xt_hi", [HALF, 2, PAD], F32R)
        xt_lo = sb("xt_lo", [HALF, 2, PAD], F32R)
        k_hi = sb("k_hi", [HALF, 2, PAD], F32R)
        k_lo = sb("k_lo", [HALF, 2, PAD], F32R)
        q_hi = sb("q_hi", [HALF, 2, PAD], F32R)
        q_lo = sb("q_lo", [HALF, 2, PAD], F32R)
        q_st = two("q_st", [128, 2, PPC, PAD], F32R)
        k_st = two("k_st", [128, 2, HPC, PAD], F32R)
        v_sb = two("v_sb", [TILE, 2, HEADS, 32])
        row_max = sb("row_max", [TILE, 2, HEADS])
        neg_max = sb("neg_max", [TILE, 2 * HEADS], F32R)
        max_cols = sb("max_cols", [TILE, 4, 128])
        pt = sb("pt", [TILE, HEADS, PCOLS])
        ot = sb("ot", [128, GROUPS, PAD])
        sum_inv = sb("sum_inv", [TILE, 2, HEADS])
        o_tok = sb("o_tok", [TILE, 2, HID])
        o_hi = sb("o_hi", [HALF, 2, PAD], F32R)
        o_lo = sb("o_lo", [HALF, 2, PAD], F32R)
        h2 = two("h2", [TILE, 2, HID])
        stats2 = sb("stats2", [TILE, 2, 6])
        mean_var2 = sb("mean_var2", [TILE, 2, 2])
        var_eps2 = sb("var_eps2", [TILE, 2])
        rstd2 = sb("rstd2", [TILE, 2])
        xn2 = sb("xn2", [TILE, 2, HID])
        xt2_hi = two("xt2_hi", [HALF, 2, PAD], F32R)
        xt2_lo = two("xt2_lo", [HALF, 2, PAD], F32R)
        gate_sum = sb("gate_sum", [HALF, 2])
        logit = sb("logit", [1, EXPERTS])
        neg_top = sb("neg_top", [1, 1])
        gate_exp = sb("gate_exp", [1, EXPERTS])
        gate_den = sb("gate_den", [1, 1])
        gate_prob = sb("gate_prob", [1, 1])
        below_top = sb("below_top", [1, EXPERTS])
        second = sb("second", [1, 1])
        choice = sb("choice", [1, 1], I32)
        weight = two("weight", [TILE, 1])
        w1_sb = two("w1_sb", [HALF, 2, 2, FFN], F32R)
        w2_sb = two("w2_sb", [128, W2COLS])
        b2_sb = two("b2_sb", [TILE, HID])
        act_sb = sb("act_sb", [128, FCH, PAD])
        y_sb = sb("y_sb", [TILE, 2, HID])
        out_sb = two("out_sb", [TILE, 2, HID])

        score = [ctx.enter_context(nc.psum_tensor(f"score{i}", [128, 2, 512], F32)) for i in range(2)]
        dense = [ctx.enter_context(nc.psum_tensor(f"dense{i}", [128, 512], F32)) for i in range(2)]
        turned = ctx.enter_context(nc.psum_tensor("turned", [128, 512], F32))
        mixed = ctx.enter_context(nc.psum_tensor("mixed", [128, 512], F32))

        s_small = sem("s_small")
        s_big = [sem(f"s_big{i}") for i in range(2)]
        s_zero = sem("s_zero")
        s_const = sem("s_const")
        s_split = sem("s_split")
        s_saved = [sem(f"s_saved{i}") for i in range(2)]
        x_in = [sem(f"x_in{i}") for i in range(2)]
        patch_mm = sem("patch_mm")
        h_ready = sem("h_ready")
        var_ready = sem("var_ready")
        rstd_ready = sem("rstd_ready")
        xn_ready = sem("xn_ready")
        hb_ready = sem("hb_ready")
        xt_mm = sem("xt_mm")
        xt_hi_ready = sem("xt_hi_ready")
        xt_lo_ready = sem("xt_lo_ready")
        qk_mm = sem("qk_mm")
        qk_hi_ready = sem("qk_hi_ready")
        qk_lo_ready = sem("qk_lo_ready")
        stacked = [sem(f"stacked{i}") for i in range(2)]
        v_mm = sem("v_mm")
        v_ready = sem("v_ready")
        smax_mm = sem("smax_mm")
        smax_done = sem("smax_done")
        negmax_ready = sem("negmax_ready")
        max_cols_ready = sem("max_cols_ready")
        max_mm = sem("max_mm")
        max_ready = sem("max_ready")
        score_mm = sem("score_mm")
        exp_done = sem("exp_done")
        causal_done = sem("causal_done")
        pv_mm = sem("pv_mm")
        ot_ready = sem("ot_ready")
        otr_mm = sem("otr_mm")
        inv_ready = sem("inv_ready")
        o_ready = sem("o_ready")
        o2_mm = sem("o2_mm")
        o_hi_ready = sem("o_hi_ready")
        o_lo_ready = sem("o_lo_ready")
        proj_mm = sem("proj_mm")
        h2_ready = sem("h2_ready")
        var2_ready = sem("var2_ready")
        rstd2_ready = sem("rstd2_ready")
        xn2_ready = sem("xn2_ready")
        xt2_mm = sem("xt2_mm")
        xt2_hi_ready = sem("xt2_hi_ready")
        xt2_lo_ready = sem("xt2_lo_ready")
        gsum_mm = sem("gsum_mm")
        gsum_ready = sem("gsum_ready")
        logit_mm = sem("logit_mm")
        logit_ready = sem("logit_ready")
        top_ready = sem("top_ready")
        gexp_done = sem("gexp_done")
        prob_ready = sem("prob_ready")
        choice_ready = sem("choice_ready")
        choice_read = sem("choice_read")
        weight_mm = sem("weight_mm")
        weight_ready = sem("weight_ready")
        w_in = [sem(f"w_in{i}") for i in range(2)]
        up_mm = sem("up_mm")
        gelu_done = sem("gelu_done")
        down_mm = sem("down_mm")
        y_ready = sem("y_ready")
        out_ready = sem("out_ready")
        stored = [sem(f"stored{i}") for i in range(2)]
        dve_step = sem("dve_step")
        unused = sem("unused")

        def score_slot(image, k):
            return (11 * image.par + k) % 2

        stage = pt[:, :, :].rearrange("p h c -> p (h c)")

        def staged(i):
            return stage[0:HALF, i * 2 * FFN:(i + 1) * 2 * FFN].rearrange("p (c n) -> p c n", c=2)

        def stand_alone(engine):
            engine.sem_inc(unused, 1)

        block = ctx.enter_context(nc.Block())

        @block.sync
        def _(sp):
            sp.dma_start(staged(0), attn_w.rearrange("(c p) n -> p c n", c=2)).then_inc(s_big[0], 16)
            sp.dma_start(x_sb[0][:], x[0]).then_inc(x_in[0], 16)
            sp.dma_start(tok_w_sb[:], tok_w).then_inc(s_small, 16)
            sp.dma_start(tok_bias_sb[:, 0, :], tok_bias.partition_broadcast(TILE)).then_inc(s_small, 16)
            sp.dma_start(tok_bias_sb[:, 1, :], tok_bias.partition_broadcast(TILE)).then_inc(s_small, 16)
            sp.dma_start(proj_bias_sb[:], proj_bias.partition_broadcast(TILE)).then_inc(s_small, 16)
            sp.dma_start(gate_w_sb[:], gate_w[1]).then_inc(s_small, 16)
            sp.wait_ge(s_small, 80)
            sp.dma_start(tok_bias_sb[0:1, 0, :], gate_w[0]).then_inc(s_small, 16)
            sp.dma_start(x_sb[1][:], x[1]).then_inc(x_in[1], 16)
            for e in range(EXPERTS):
                i = (e + 1) % 2
                if e >= 1:
                    sp.wait_ge(s_split, 2 * e)
                sp.dma_start(staged(i), w1[e].rearrange("(c p) n -> p c n", c=2)).then_inc(s_big[i], 16)
            for e in range(EXPERTS):
                sp.wait_ge(s_split, 2 * (e + 2))
                sp.dma_start(w1_split[e], w1_sb[e % 2][:].bitcast(F32).rearrange("p c s n -> p (c s n)")).then_inc(s_saved[e % 2], 16)
            sp.wait_ge(s_saved[0], 32)
            sp.wait_ge(s_saved[1], 16)

            def load_x(a):
                sp.wait_ge(patch_mm, a.back(2).count(2, 2))
                sp.dma_start(x_sb[a.par][:], x[a.index()]).then_inc(x_in[a.par], 16)

            def load_expert(c):
                sp.wait_ge(choice_ready, c.count(1, 1))
                stand_alone(sp)
                e = sp.value_load(choice[0:1, 0:1], min_val=0, max_val=EXPERTS - 1)
                if c.trip is not None or c.first >= 2:
                    sp.wait_ge(out_ready, c.back(2).count(2, 2))
                sp.dma_start(w1_sb[c.par][:].bitcast(F32).rearrange("p c s n -> p (c s n)"), w1_split[e]).then_inc(w_in[c.par], 16)
                sp.dma_start(w2_sb[c.par][:], w2b1[e]).then_inc(w_in[c.par], 16)
                sp.dma_start(b2_sb[c.par][:], b2[e].partition_broadcast(TILE)).then_inc(w_in[c.par], 16)
                sp.sem_inc(choice_read, 1)

            def stack(a, half):
                sp.wait_ge(qk_lo_ready, a.count(4, 2 * half + 2))
                if half == 0 and (a.trip is not None or a.first >= 2):
                    stand_alone(sp)
                    sp.wait_ge(score_mm, a.back(2).count(6, 6))
                stand_alone(sp)
                for i in range(PPC):
                    if half == 0:
                        for z in range(2):
                            row = 32 * i + HD * z
                            for block, src in enumerate((k_hi, k_hi, k_lo)):
                                to = 32 * block + HD * z
                                sp.dma_start(k_st[a.par][to:to + HD, :, 2 * i + z, :].bitcast(F32),
                                             src[row:row + HD, :, :].bitcast(F32)).then_inc(stacked[a.par], 16)
                    else:
                        for block, src in enumerate((q_hi, q_lo, q_hi)):
                            sp.dma_start(q_st[a.par][32 * block:32 * block + 32, :, i, :].bitcast(F32),
                                         src[32 * i:32 * i + 32, :, :].bitcast(F32)).then_inc(stacked[a.par], 16)

            def store(d):
                for j in range(2):
                    sp.wait_ge(out_ready, d.count(2, j + 1))
                    rows = TILE - j
                    sp.dma_start(out[d.index(), j * TILE:j * TILE + rows, :],
                                 out_sb[d.par][0:rows, j, :]).then_inc(stored[d.par], 16)

            def turn(n, trip):
                x2, a, c, d = (Image(n + k, trip) for k in (2, 1, -1, -2))
                if x2.real() and n >= 0:
                    load_x(x2)
                if a.real():
                    stack(a, 0)
                    stack(a, 1)
                if c.real():
                    load_expert(c)
                if d.real():
                    store(d)

            run_turns(sp, turn)
            for s in stored:
                sp.wait_ge(s, 16 * IMAGES)

        @block.gpsimd
        def _(pool):
            g = nc.gpsimd
            g.memset(ident[:], 0.0).then_inc(s_zero, 1)
            g.memset(ident_b[:], 0.0).then_inc(s_zero, 1)
            g.memset(causal0[:], 0.0).then_inc(s_zero, 1)
            g.memset(causal1[:], 0.0).then_inc(s_zero, 1)
            for i in range(2):
                g.memset(k_st[i][0:MROW].bitcast(F32), 0.0).then_inc(s_const, 1)
            g.memset(pick_max[:], 0.0).then_inc(s_zero, 1)
            g.memset(real_tok[:], 1.0).then_inc(s_zero, 1)
            g.memset(ones_row[:], 1.0).then_inc(s_const, 1)
            g.memset(minus_half[:], -0.5).then_inc(s_const, 1)
            g.memset(max_cols[:], 0.0).then_inc(s_const, 1)
            for i in range(2):
                g.memset(v_sb[i][:], 0.0).then_inc(s_zero, 1)
            pool.wait_ge(s_zero, 8)
            g.affine_select(out=ident[:], in_=ident[:], compare_op=ALU.not_equal, fill=1.0, base=0,
                            pattern=[[-1, 128]], channel_multiplier=1).then_inc(s_const, 1)
            g.affine_select(out=ident_b[:], in_=ident_b[:], compare_op=ALU.not_equal, fill=1.0, base=0,
                            pattern=[[-1, TILE]], channel_multiplier=1).then_inc(s_const, 1)
            g.affine_select(out=causal0[:], in_=causal0[:], compare_op=ALU.is_ge, fill=BIG, base=0,
                            pattern=[[-1, KEYS0]], channel_multiplier=1).then_inc(s_const, 1)
            g.affine_select(out=causal1[:], in_=causal1[:], compare_op=ALU.is_ge, fill=BIG, base=1,
                            pattern=[[-1, KEYS0]], channel_multiplier=1).then_inc(s_const, 1)
            g.affine_select(out=real_tok[:], in_=real_tok[:], compare_op=ALU.not_equal, fill=0.0,
                            base=-(TILE - 1 + 1), pattern=[[1, 2]], channel_multiplier=1).then_inc(s_const, 1)
            for part in range(2):
                g.affine_select(out=pick_max[:], in_=pick_max[:], compare_op=ALU.not_equal,
                                fill=1.0, base=-MROW - HPC * part, pattern=[[-1, HPC]],
                                channel_multiplier=1).then_inc(s_zero, 1)
                pool.wait_ge(s_zero, 9 + part)
            for i in range(2):
                g.memset(v_sb[i][:, :, :, HD:HD + 1], 1.0).then_inc(s_const, 1)

            def rstd_of(image, ready, src, done, dst):
                pool.wait_ge(ready, image.count(1, 1))
                g.tensor_tensor(dst[:], src[:], minus_half[:], ALU.pow).then_inc(done, 1)

            def residual_bias(a):
                pool.wait_ge(h_ready, a.count(2, 2))
                if a.trip is not None or a.first >= 2:
                    pool.wait_ge(h2_ready, a.back(2).count(2, 2))
                g.tensor_tensor(h_bias[a.par][:], h_sb[:],
                                proj_bias_sb[:].unsqueeze(1).to_broadcast([TILE, 2, HID]), ALU.add).then_inc(hb_ready, 1)

            def hide_future(b, s):
                pool.wait_ge(exp_done, b.count(6, s + 1))
                stand_alone(pool)
                v = pt[:, 2 * s:2 * s + 2, 0:2 * KEYS0].rearrange("p h (r q) -> p h r q", r=2)
                g.affine_select(out=v, in_=v, compare_op=ALU.is_ge, fill=0.0, base=-1,
                                pattern=[[0, 2], [1, 2], [1, KEYS0]], channel_multiplier=-1).then_inc(causal_done, 1)

            pool.wait_ge(s_small, 96)
            pool.wait_ge(s_const, 12)

            def turn(n, trip):
                a, b, c = (Image(n + k, trip) for k in (1, 0, -1))
                if a.real():
                    rstd_of(a, var_ready, var_eps, rstd_ready, rstd)
                if c.real():
                    rstd_of(c, var2_ready, var_eps2, rstd2_ready, rstd2)
                if a.real():
                    residual_bias(a)
                if b.real():
                    for s in range(6):
                        hide_future(b, s)

            run_turns(pool, turn)

        @block.scalar
        def _(act):
            act.wait_ge(s_zero, 10)
            for i in range(2):
                for c in range(2):
                    nc.scalar.activation(k_st[i][MROW:128, c, :, :],
                                         pick_max[MROW:128, :].unsqueeze(2).to_broadcast([128 - MROW, HPC, PAD]),
                                         ACT.Copy).then_inc(s_const, 1)

            def hi(image, dst, src, ready, per, k, done):
                act.wait_ge(ready, image.count(per, k))
                nc.scalar.activation(dst, src, ACT.Copy).then_inc(done, 1)

            def both(bank):
                return bank[0:HALF, 0:2 * PAD].rearrange("p (c t) -> p c t", c=2)

            def xt(a):
                if a.trip is not None or a.first >= 1:
                    act.wait_ge(v_mm, a.back(1).count(2, 2))
                hi(a, xt_hi[:], both(turned), xt_mm, 1, 1, xt_hi_ready)

            def qk(a, u):
                dst = (k_hi if u < 2 else q_hi)[:, u % 2, :]
                if u == 0 and (a.trip is not None or a.first >= 1):
                    act.wait_ge(stacked[1 - a.par], a.back(1).turns(16 * STACK_DMAS, 16 * STACK_DMAS))
                hi(a, dst, dense[u % 2][0:HALF, 0:PAD], qk_mm, 4, u + 1, qk_hi_ready)

            def values(a, t):
                act.wait_ge(v_mm, a.count(2, t + 1))
                if t == 0 and (a.trip is not None or a.first >= 2):
                    act.wait_ge(pv_mm, a.back(2).count(GROUPS, GROUPS))
                nc.scalar.activation(v_sb[a.par][:, t, :, 0:HD],
                                     dense[t][0:TILE, 0:HID].rearrange("p (h d) -> p h d", h=HEADS),
                                     ACT.Copy).then_inc(v_ready, 1)

            def max_rows(b):
                act.wait_ge(max_mm, b.count(1, 1))
                rows = mixed[MROW:128, 0:2 * PAD].rearrange("p (c t) -> p c t", c=2)
                nc.scalar.activation(q_st[b.par][MROW:128, :, :, :],
                                     rows.unsqueeze(2).to_broadcast([128 - MROW, 2, PPC, PAD]),
                                     ACT.Copy).then_inc(max_ready, 1)

            def exps(b, s):
                act.wait_ge(score_mm, b.count(6, s + 1))
                if s % 2 == 0 and (b.trip is not None or b.first >= 1):
                    act.wait_ge(pv_mm, b.back(1).count(GROUPS, s // 2 + 1))
                nc.scalar.activation(pt[:, 2 * s:2 * s + 2, :],
                                     score[score_slot(b, 5 + s)][0:TILE, :, 2 * PAD - PCOLS:2 * PAD],
                                     ACT.Exp, scale=HD ** -0.5).then_inc(exp_done, 1)

            def mixed_out(b, g):
                act.wait_ge(pv_mm, b.count(GROUPS, g + 1))
                if g == 0 and (b.trip is not None or b.first >= 1):
                    act.wait_ge(otr_mm, b.back(1).count(2, 2))
                nc.scalar.activation(ot[:, g, :], mixed[:, 0:PAD], ACT.Copy).then_inc(ot_ready, 1)

            def o_high(c):
                if c.trip is not None or c.first >= 1:
                    act.wait_ge(proj_mm, c.back(1).count(2, 2))
                hi(c, o_hi[:], both(mixed), o2_mm, 1, 1, o_hi_ready)

            def xt2(c):
                if c.trip is not None or c.first >= 2:
                    act.wait_ge(up_mm, c.back(2).count(FCH, FCH))
                hi(c, xt2_hi[c.par][:], both(mixed), xt2_mm, 1, 1, xt2_hi_ready)

            def gate_exps(c):
                act.wait_ge(top_ready, c.count(1, 1))
                nc.scalar.activation(gate_exp[:], logit[:], ACT.Exp, bias=neg_top[:],
                                     accum_out=gate_den[:]).then_inc(gexp_done, 1)

            def gelu(d, m):
                act.wait_ge(up_mm, d.count(FCH, m + 1))
                if m == 0 and (d.trip is not None or d.first >= 1):
                    act.wait_ge(down_mm, d.back(1).count(2, 2))
                nc.scalar.activation(act_sb[:, m, :], dense[m % 2][:, 0:PAD], ACT.Gelu,
                                     bias=w2_sb[d.par][:, FCH * HID + m:FCH * HID + m + 1]).then_inc(gelu_done, 1)

            def turn(n, trip):
                a, b, c, d = (Image(n + k, trip) for k in (1, 0, -1, -2))
                A, B, C, D = a.real(), b.real(), c.real(), d.real()
                if C:
                    mixed_out(c, 2)
                    o_high(c)
                if D:
                    gelu(d, 0)
                if A:
                    xt(a)
                if D:
                    gelu(d, 1)
                if A:
                    qk(a, 0), qk(a, 1)
                    qk(a, 2), qk(a, 3)
                if D:
                    gelu(d, 2), gelu(d, 3)
                if A:
                    values(a, 0), values(a, 1)
                if B:
                    max_rows(b)
                if D:
                    gelu(d, 4)
                if C:
                    xt2(c)
                if D:
                    gelu(d, 5)
                if B:
                    exps(b, 0)
                if C:
                    gate_exps(c)
                if B:
                    exps(b, 1)
                    exps(b, 2)
                    mixed_out(b, 0)
                    exps(b, 3), exps(b, 4)
                    mixed_out(b, 1)
                    exps(b, 5)

            run_turns(act, turn)

        @block.vector
        def _(dve):
            v = nc.vector
            for i in range(EXPERTS + 1):
                half = i % 2
                dve.wait_ge(s_big[half], 16 * (i // 2 + 1))
                dst = attn_w_sb if i == 0 else w1_sb[(i - 1) % 2]
                if i == EXPERTS:
                    dve.wait_ge(s_saved[0], 16)
                v.tensor_copy(dst[:, :, 0, :], staged(half)).then_inc(s_split, 1)
                dve.wait_ge(s_split, 2 * i + 1)
                v.tensor_tensor(dst[:, :, 1, :], staged(half), dst[:, :, 0, :].bitcast(F32),
                                ALU.subtract).then_inc(s_split, 1)
            dve.wait_ge(s_const, 16)
            dve.wait_ge(s_small, 96)

            def low(image, dst, src, high, ready, per, k, done):
                dve.wait_ge(ready, image.count(per, k))
                v.tensor_tensor(dst, src, high.bitcast(F32), ALU.subtract).then_inc(done, 1)

            def both(bank):
                return bank[0:HALF, 0:2 * PAD].rearrange("p (c t) -> p c t", c=2)

            class Steps:
                per_turn = 12

                def __init__(self):
                    self.n, self.trip = 0, None

                def link(self, instruction):
                    instruction.then_inc(dve_step, 1)
                    self.n += 1
                    dve.wait_ge(dve_step, self.n if self.trip is None else self.trip * (2 * self.per_turn) + self.n)

            steps = Steps()
            link = steps.link

            def block_max(b, k):
                dve.wait_ge(smax_mm, b.count(5, k + 1))
                if k == 0 and (b.trip is not None or b.first >= 1):
                    dve.wait_ge(max_cols_ready, b.back(1).count(1, 1))
                slot = score[score_slot(b, k)]
                if k < 2:
                    heads = 4 - 2 * k
                    v.reduce_max(row_max[:, 0, 8 * k:8 * k + 2 * heads].rearrange("p (z h) -> p z h", z=2),
                                 slot[0:TILE, :, 0:heads * KEYS0].rearrange("p z (h k) -> p z h k", h=heads),
                                 AX_X).then_inc(smax_done, 1)
                else:
                    h = 4 * (k - 2)
                    v.reduce_max(row_max[:, 1, h:h + 4].rearrange("p (z h) -> p z h", z=2),
                                 slot[0:TILE, :, 0:2 * PAD].rearrange("p z (h k) -> p z h k", h=2),
                                 AX_X).then_inc(smax_done, 1)

            def normalise(c, j):
                bank = (mixed, turned)[j]
                view = bank[0:TILE, 0:HEADS * 32].rearrange("p (h e) -> p h e", h=HEADS)
                dve.wait_ge(otr_mm, c.count(2, j + 1))
                if j == 0 and (c.trip is not None or c.first >= 1):
                    dve.wait_ge(o2_mm, c.back(1).count(1, 1))
                v.reciprocal(sum_inv[:, j, :], view[:, :, HD]).then_inc(inv_ready, 1)
                dve.wait_ge(inv_ready, c.count(2, j + 1))
                v.tensor_tensor(o_tok[:, j, :].rearrange("p (h e) -> p h e", h=HEADS), view[:, :, 0:HD],
                                sum_inv[:, j, :].unsqueeze(2).to_broadcast([TILE, HEADS, HD]),
                                ALU.mult).then_inc(o_ready, 1)

            def embed(a, t):
                dve.wait_ge(patch_mm, a.count(2, t + 1))
                if t == 0 and (a.trip is not None or a.first >= 1):
                    dve.wait_ge(hb_ready, a.back(1).count(1, 1))
                v.tensor_tensor(h_sb[:, t, :], dense[t][0:TILE, 0:HID], tok_bias_sb[:, t, :], ALU.add).then_inc(h_ready, 1)
                dve.wait_ge(h_ready, a.count(2, t + 1))
                link(v.bn_stats(stats[:, t, :], h_sb[:, t, :]))
                stand_alone(dve)
                link(v.bn_aggr(mean_var[:, t, :], stats[:, t, :]))

            def residual(c, j):
                dve.wait_ge(proj_mm, c.count(2, j + 1))
                if j == 0:
                    dve.wait_ge(hb_ready, c.count(1, 1))
                v.tensor_tensor(h2[c.par][:, j, :], dense[j][0:TILE, 0:HID], h_bias[c.par][:, j, :],
                                ALU.add).then_inc(h2_ready, 1)
                dve.wait_ge(h2_ready, c.count(2, j + 1))
                link(v.bn_stats(stats2[:, j, :], h2[c.par][:, j, :]))
                stand_alone(dve)
                link(v.bn_aggr(mean_var2[:, j, :], stats2[:, j, :]))

            def variance(dst, mv, done):
                v.tensor_scalar(dst[:], mv[:, :, 1], EPS, None, ALU.add).then_inc(done, 1)

            def layer_norm(image, dst, src, mv, rs, ready, done, used):
                dve.wait_ge(ready, image.count(1, 1))
                if image.trip is not None or image.first >= 1:
                    sem_used, per = used
                    dve.wait_ge(sem_used, image.back(1).count(per, per))
                for t in range(2):
                    v.tensor_scalar(dst[:, t, :], src[:, t, :], mv[:, t, 0:1], rs[:, t:t + 1],
                                    ALU.subtract, ALU.mult).then_inc(done, 1)

            def spread_max(b):
                m = row_max[:].rearrange("p j h -> p (j h)")
                dve.wait_ge(smax_done, b.count(5, 5))
                if b.trip is not None or b.first >= 1:
                    dve.wait_ge(max_mm, b.back(1).count(1, 1))
                v.tensor_scalar(neg_max[:], m, -1.0, None, ALU.mult).then_inc(negmax_ready, 1)
                dve.wait_ge(negmax_ready, b.count(1, 1))
                grouped = "p (g h) -> p g h"
                link(v.tensor_copy(max_cols[:, :, MROW:MROW + HPC],
                                   neg_max[:].bitcast(F32).rearrange(grouped, g=4)))
                v.scalar_tensor_tensor(out=max_cols[:, :, MROW + HPC:MROW + 2 * HPC],
                                       in0=m.rearrange(grouped, g=4), scalar=-1.0,
                                       in1=neg_max[:].bitcast(F32).rearrange(grouped, g=4),
                                       op0=ALU.mult, op1=ALU.subtract).then_inc(max_cols_ready, 1)

            def gate_sums(c):
                dve.wait_ge(gsum_mm, c.count(1, 1))
                v.tensor_copy(gate_sum[:], turned[0:HALF, 0:2]).then_inc(gsum_ready, 1)

            def gate(c):
                dve.wait_ge(logit_mm, c.count(1, 1))
                if c.trip is not None or c.first >= 1:
                    dve.wait_ge(gexp_done, c.back(1).count(1, 1))
                v.tensor_scalar(logit[:], turned[0:1, 0:EXPERTS], 1.0 / TOKENS, None, ALU.mult).then_inc(logit_ready, 1)
                dve.wait_ge(logit_ready, c.count(1, 1))
                link(v.reduce_max(second[:], logit[:], AX_X))
                v.tensor_scalar(neg_top[:], second[:], -1.0, None, ALU.mult).then_inc(top_ready, 1)
                link(v.tensor_scalar(below_top[:], logit[:], second[:], None, ALU.is_lt))
                link(v.tensor_scalar(second[:], below_top[:, 1:2], 1.0, None, ALU.add))
                if c.trip is not None or c.first >= 1:
                    dve.wait_ge(choice_read, c.back(1).count(1, 1))
                v.tensor_tensor(choice[:], second[:], below_top[:, 0:1], ALU.mult).then_inc(choice_ready, 1)

            def gate_weight(c):
                dve.wait_ge(gexp_done, c.count(1, 1))
                v.reciprocal(gate_prob[:], gate_den[:]).then_inc(prob_ready, 1)

            def spread_weight(c):
                dve.wait_ge(weight_mm, c.count(1, 1))
                v.tensor_copy(weight[c.par][:], turned[0:TILE, 0:1]).then_inc(weight_ready, 1)

            def finish(d, j):
                dve.wait_ge(down_mm, d.count(2, j + 1))
                if j == 0:
                    dve.wait_ge(w_in[d.par], d.turns(48, 48))
                    dve.wait_ge(weight_ready, d.count(1, 1))
                    if d.trip is not None or d.first >= 1:
                        dve.wait_ge(out_ready, d.back(1).count(2, 2))
                    if d.trip is not None or d.first >= 2:
                        dve.wait_ge(stored[d.par], d.turns(32, 0))
                v.tensor_tensor(y_sb[:, j, :], dense[j][0:TILE, 0:HID], b2_sb[d.par][:], ALU.add).then_inc(y_ready, 1)
                dve.wait_ge(y_ready, d.count(2, j + 1))
                v.scalar_tensor_tensor(out=out_sb[d.par][:, j, :], in0=y_sb[:, j, :], scalar=weight[d.par][:, 0:1],
                                       in1=h2[d.par][:, j, :], op0=ALU.mult, op1=ALU.add).then_inc(out_ready, 1)

            def qk_low(a, u):
                dst, high = ((k_lo, k_hi) if u < 2 else (q_lo, q_hi))
                dst, high = dst[:, u % 2, :], high[:, u % 2, :]
                low(a, dst, dense[u % 2][0:HALF, 0:PAD], high, qk_hi_ready, 4, u + 1, qk_lo_ready)

            def turn(n, trip):
                a, b, c, d = (Image(n + k, trip) for k in (1, 0, -1, -2))
                A, B, C, D = a.real(), b.real(), c.real(), d.real()
                if A:
                    embed(a, 0)
                    embed(a, 1)
                    variance(var_eps, mean_var, var_ready)
                if C:
                    normalise(c, 0), normalise(c, 1)
                if A:
                    layer_norm(a, xn, h_sb, mean_var, rstd, rstd_ready, xn_ready, (xt_mm, 1))
                if B:
                    block_max(b, 0)
                    block_max(b, 1)
                if C:
                    low(c, o_lo[:], both(mixed), o_hi[:], o_hi_ready, 1, 1, o_lo_ready)
                if A:
                    low(a, xt_lo[:], both(turned), xt_hi[:], xt_hi_ready, 1, 1, xt_lo_ready)
                if B:
                    block_max(b, 2)
                if C:
                    residual(c, 0), residual(c, 1)
                    variance(var_eps2, mean_var2, var2_ready)
                if A:
                    qk_low(a, 0), qk_low(a, 1)
                if B:
                    block_max(b, 3)
                if A:
                    qk_low(a, 2), qk_low(a, 3)
                if B:
                    block_max(b, 4)
                    spread_max(b)
                if C:
                    layer_norm(c, xn2, h2[c.par], mean_var2, rstd2, rstd2_ready, xn2_ready, (gsum_mm, 1))
                    low(c, xt2_lo[c.par][:], both(mixed), xt2_hi[c.par][:], xt2_hi_ready, 1, 1, xt2_lo_ready)
                    gate_sums(c)
                    gate(c)
                    gate_weight(c)
                if D:
                    finish(d, 0)
                if C:
                    spread_weight(c)
                if D:
                    finish(d, 1)

            start = []

            def enter(trip):
                start.append(steps.n)
                steps.trip = trip

            def leave(trips):
                steps.trip = None
                assert steps.n - start[0] == 2 * steps.per_turn, (steps.n - start[0]) / 2
                steps.n += 2 * steps.per_turn * (trips - 1)

            run_turns(dve, turn, enter, leave)

        @block.tensor
        def _(pe):
            mm = nc.tensor.matmul
            turns = BankTurns(pe)
            pe.wait_ge(s_small, 96)
            pe.wait_ge(s_const, 16)
            pe.wait_ge(s_split, 2)

            def three(dst, pairs):
                ops = [p for lh, ll, rh, rl in pairs for p in ((lh, rh), (lh, rl), (ll, rh))]
                for i, (l, r) in enumerate(ops):
                    last = mm(dst, l, r, start=(i == 0), stop=(i == len(ops) - 1))
                return last

            def stacked_q(b, h, rows):
                return q_st[b.par][rows, h // HPC, h % HPC // 2, :]

            def score_max(b, k):
                slot = score_slot(b, k)
                turns.take(("score", slot), b, smax_done, 5, k + 1)
                if k == 0:
                    pe.wait_ge(stacked[b.par], b.turns(16 * STACK_DMAS, 16 * STACK_DMAS))
                for z in range(2):
                    if k < 2:
                        heads, keys, t, hidden, first = 4 - 2 * k, KEYS0, 0, causal0, 0
                        h = 8 * k + heads * z
                    else:
                        heads, keys, t, hidden, first = 2, PAD, 1, causal1, PAD - KEYS0
                        h = 4 * (k - 2) + 2 * z
                    dst = score[slot][0:TILE, z, 0:heads * keys].rearrange("p (h k) -> p h k", h=heads)
                    for i in range(0, heads, 2):
                        mm(dst[:, i:i + 2], stacked_q(b, h + i, slice(0, MROW))[:, t * TILE:(t + 1) * TILE],
                           k_st[b.par][0:MROW, (h + i) // HPC, (h + i) % HPC:(h + i) % HPC + 2, 0:keys],
                           start=(i == 0), stop=False)
                    last = mm(dst[:, :, first:first + KEYS0], ident_b[:],
                              hidden[:].unsqueeze(1).to_broadcast([TILE, heads, KEYS0]), start=False, stop=True)
                last.then_inc(smax_mm, 1)

            def turn_max(b):
                turns.take("mixed", b, max_ready, 1, 1)
                pe.wait_ge(max_cols_ready, b.count(1, 1))
                for c in range(2):
                    for j in range(2):
                        last = nc.tensor.transpose(mixed[:, c * PAD + j * TILE:c * PAD + (j + 1) * TILE],
                                                   max_cols[:, 2 * j + c, :], ident[0:TILE, 0:TILE])
                last.then_inc(max_mm, 1)

            def scores(b, s):
                slot = score_slot(b, 5 + s)
                turns.take(("score", slot), b, exp_done, 6, s + 1)
                if s == 0:
                    pe.wait_ge(max_ready, b.count(1, 1))
                for z in range(2):
                    h = 2 * s + z
                    for i, t in enumerate((1, 0)):
                        dst = score[slot][0:TILE, z, i * PAD:(i + 1) * PAD]
                        keys = slice(t * TILE, (t + 1) * TILE)
                        last = mm(dst, k_st[b.par][:, h // HPC, h % HPC, keys], stacked_q(b, h, slice(0, 128)),
                                  start=True, stop=True)
                last.then_inc(score_mm, 1)

            def mix(b, g):
                turns.take("mixed", b, ot_ready, GROUPS, g + 1)
                pe.wait_ge(causal_done, b.count(6, 2 * g + 2))
                if g == 0:
                    pe.wait_ge(v_ready, b.count(2, 2))
                for j in range(4):
                    h = 4 * g + j
                    mm(mixed[32 * j:32 * j + 32, 0:PAD], v_sb[b.par][:, 0, h, :], pt[:, h, KEYS0:PCOLS],
                       start=True, stop=False)
                    last = mm(mixed[32 * j:32 * j + 32, PAD - KEYS0:PAD], v_sb[b.par][:, 1, h, :],
                              pt[:, h, 0:KEYS0], start=False, stop=True)
                last.then_inc(pv_mm, 1)

            def turn_out(c, j):
                name, bank = (("mixed", mixed), ("turned", turned))[j]
                turns.take(name, c, o_ready, 2, j + 1)
                if j == 0:
                    pe.wait_ge(ot_ready, c.count(GROUPS, GROUPS))
                for g in range(GROUPS):
                    last = nc.tensor.transpose(bank[0:TILE, g * 128:(g + 1) * 128],
                                               ot[:, g, j * TILE:(j + 1) * TILE], ident[:])
                last.then_inc(otr_mm, 1)

            def turn_tokens(image, name, bank, src, ready, per, done, read_done):
                turns.take(name, image, read_done, 1, 1)
                pe.wait_ge(ready, image.count(per, per))
                for c in range(2):
                    for j in range(2):
                        last = nc.tensor.transpose(bank[0:HALF, c * PAD + j * TILE:c * PAD + (j + 1) * TILE],
                                                   src[:, j, c * HALF:(c + 1) * HALF], ident[0:TILE, 0:TILE])
                last.then_inc(done, 1)

            def patches(a, t):
                turns.take(f"dense{t}", a, h_ready, 2, t + 1)
                if t == 0:
                    pe.wait_ge(x_in[a.par], a.turns(16, 16))
                for k in range(KP):
                    last = mm(dense[t][0:TILE, 0:HID], x_sb[a.par][:, k, t * TILE:(t + 1) * TILE], tok_w_sb[:, k, :],
                              start=(k == 0), stop=(k == KP - 1))
                last.then_inc(patch_mm, 1)

            def weights(c, part, first, n):
                return attn_w_sb[:, c, part, first:first + n]

            def qk(a, u):
                turns.take(f"dense{u % 2}", a, qk_lo_ready, 4, u + 1)
                if u == 0:
                    pe.wait_ge(xt_lo_ready, a.count(1, 1))
                first = (HID if u < 2 else 0) + (u % 2) * HALF
                three(dense[u % 2][0:HALF, 0:PAD],
                      [(weights(c, 0, first, HALF), weights(c, 1, first, HALF), xt_hi[:, c, :], xt_lo[:, c, :])
                       for c in range(2)]).then_inc(qk_mm, 1)

            def values(a, t):
                turns.take(f"dense{t}", a, v_ready, 2, t + 1)
                tok = slice(t * TILE, (t + 1) * TILE)
                three(dense[t][0:TILE, 0:HID],
                      [(xt_hi[:, c, tok], xt_lo[:, c, tok], weights(c, 0, 2 * HID, HID), weights(c, 1, 2 * HID, HID))
                       for c in range(2)]).then_inc(v_mm, 1)

            def project(c, j):
                turns.take(f"dense{j}", c, h2_ready, 2, j + 1)
                if j == 0:
                    pe.wait_ge(o_lo_ready, c.count(1, 1))
                tok = slice(j * TILE, (j + 1) * TILE)
                three(dense[j][0:TILE, 0:HID],
                      [(o_hi[:, k, tok], o_lo[:, k, tok], weights(k, 0, 3 * HID, HID), weights(k, 1, 3 * HID, HID))
                       for k in range(2)]).then_inc(proj_mm, 1)

            def gate_sums(c):
                turns.take("turned", c, gsum_ready, 1, 1)
                for k in range(2):
                    for j in range(2):
                        last = mm(turned[0:HALF, k:k + 1], xn2[:, j, k * HALF:(k + 1) * HALF],
                                  real_tok[:, j:j + 1], start=(j == 0), stop=(j == 1))
                last.then_inc(gsum_mm, 1)

            def logits(c):
                pe.wait_ge(gsum_ready, c.count(1, 1))
                turns.take("turned", c, logit_ready, 1, 1)
                for k in range(2):
                    last = mm(turned[0:1, 0:EXPERTS], gate_sum[:, k:k + 1], gate_w_sb[:, k, :],
                              start=(k == 0), stop=(k == 1))
                last.then_inc(logit_mm, 1)

            def spread_weight(c):
                turns.take("turned", c, weight_ready, 1, 1)
                pe.wait_ge(prob_ready, c.count(1, 1))
                mm(turned[0:TILE, 0:1], ones_row[:], gate_prob[:], start=True, stop=True).then_inc(weight_mm, 1)

            def up(d, m):
                turns.take(f"dense{m % 2}", d, gelu_done, FCH, m + 1)
                if m == 0:
                    pe.wait_ge(w_in[d.par], d.turns(48, 48))
                    pe.wait_ge(xt2_lo_ready, d.count(1, 1))
                cols = slice(m * 128, (m + 1) * 128)
                three(dense[m % 2][:, 0:PAD],
                      [(w1_sb[d.par][:, k, 0, cols], w1_sb[d.par][:, k, 1, cols], xt2_hi[d.par][:, k, :],
                        xt2_lo[d.par][:, k, :]) for k in range(2)]).then_inc(up_mm, 1)

            def down(d, j):
                turns.take(f"dense{j}", d, y_ready, 2, j + 1)
                if j == 0:
                    pe.wait_ge(gelu_done, d.count(FCH, FCH))
                for m in range(FCH):
                    last = mm(dense[j][0:TILE, 0:HID], act_sb[:, m, j * TILE:(j + 1) * TILE],
                              w2_sb[d.par][:, m * HID:(m + 1) * HID], start=(m == 0), stop=(m == FCH - 1))
                last.then_inc(down_mm, 1)

            def turn(n, trip):
                a, b, c, d = (Image(n + k, trip) for k in (1, 0, -1, -2))
                A, B, C, D = a.real(), b.real(), c.real(), d.real()
                if A:
                    patches(a, 0)
                if C:
                    mix(c, 2)
                if A:
                    patches(a, 1)
                if C:
                    turn_out(c, 0), turn_out(c, 1)
                if B:
                    score_max(b, 0)
                    score_max(b, 1)
                if C:
                    turn_tokens(c, "mixed", mixed, o_tok, o_ready, 2, o2_mm, o_lo_ready)
                if D:
                    up(d, 0)
                if B:
                    score_max(b, 2)
                if A:
                    turn_tokens(a, "turned", turned, xn, xn_ready, 2, xt_mm, xt_lo_ready)
                if D:
                    up(d, 1)
                if C:
                    project(c, 0), project(c, 1)
                if A:
                    qk(a, 0), qk(a, 1)
                if B:
                    score_max(b, 3)
                if A:
                    qk(a, 2), qk(a, 3)
                if B:
                    score_max(b, 4)
                if D:
                    up(d, 2), up(d, 3)
                if A:
                    values(a, 0), values(a, 1)
                if B:
                    turn_max(b)
                if D:
                    up(d, 4)
                if C:
                    turn_tokens(c, "mixed", mixed, xn2, xn2_ready, 2, xt2_mm, xt2_lo_ready)
                    gate_sums(c)
                if D:
                    up(d, 5)
                if B:
                    scores(b, 0)
                if C:
                    logits(c)
                if B:
                    scores(b, 1)
                if D:
                    down(d, 0)
                if B:
                    scores(b, 2)
                if C:
                    spread_weight(c)
                if B:
                    mix(b, 0)
                    scores(b, 3), scores(b, 4)
                if D:
                    down(d, 1)
                if B:
                    mix(b, 1)
                    scores(b, 5)

            def enter(trip):
                turns.trip = trip

            run_turns(pe, turn, enter, turns.leave)


def kernel(x, cls_tok, L0_tok_W_proj, L0_tok_b_proj, L0_attn_w_attn, L0_attn_w_proj, L0_attn_b_proj,
           L0_ffn_Wg, L0_ffn_W1, L0_ffn_b1, L0_ffn_W2, L0_ffn_b2):
    import numpy as np
    import concourse.bacc as bacc
    from concourse.bass_utils import run_bass_kernel_spmd

    cut = np.asarray(x).reshape(IMAGES, GRID, PATCH, GRID, PATCH, CH).transpose(0, 2, 4, 5, 1, 3)
    cols = np.zeros((IMAGES, 128, KP, PAD), np.float32)
    cols[:, :, :, 1:TOKENS] = cut.reshape(IMAGES, 128, KP, GRID * GRID)
    arrays = {
        "x_cols": cols,
        "tok_w": np.ascontiguousarray(np.asarray(L0_tok_W_proj).reshape(128, KP, HID)),
        "tok_bias": np.asarray(L0_tok_b_proj),
        "attn_w": np.concatenate([np.asarray(L0_attn_w_attn), np.asarray(L0_attn_w_proj)], axis=1),
        "proj_bias": np.asarray(L0_attn_b_proj),
        "cls": np.asarray(cls_tok).reshape(1, HID),
        "gate_w": np.ascontiguousarray(np.asarray(L0_ffn_Wg).reshape(EXPERTS, 2, HALF).transpose(2, 1, 0)),
        "w1": np.asarray(L0_ffn_W1),
        "w2b1": np.concatenate([
            np.asarray(L0_ffn_W2).reshape(EXPERTS, FCH, 128, HID).transpose(0, 2, 1, 3).reshape(EXPERTS, 128, FCH * HID),
            np.asarray(L0_ffn_b1).reshape(EXPERTS, FCH, 128).transpose(0, 2, 1)], axis=2),
        "b2": np.asarray(L0_ffn_b2),
    }
    nc = bacc.Bacc("TRN2", target_bir_lowering=False, num_devices=1)
    aps = {k: nc.dram_tensor(k, v.shape, F32, kind="ExternalInput").ap() for k, v in arrays.items()}
    out = nc.dram_tensor("out", (IMAGES, TOKENS, HID), F32, kind="ExternalOutput").ap()
    vit_tower(nc, aps["x_cols"], aps["tok_w"], aps["tok_bias"], aps["attn_w"], aps["proj_bias"],
              (aps["cls"], aps["gate_w"]), aps["w1"], aps["w2b1"], aps["b2"], out)
    result = run_bass_kernel_spmd(nc, [arrays], core_ids=[0])
    return result.results[0]["out"]
```

```python
import concourse.bass as bass
from concourse import mybir
from contextlib import ExitStack

F32 = mybir.dt.float32
F32R = mybir.dt.float32r
BF16 = mybir.dt.bfloat16
I32 = mybir.dt.int32
ALU = mybir.AluOpType
ACT = mybir.ActivationFunctionType
AX_X = mybir.AxisListType.X

IMAGES, GRID, PATCH, CH = 64, 14, 16, 3
HID, HEADS, EXPERTS, FFN = 192, 12, 3, 768
HD = HID // HEADS
TOKENS = GRID * GRID + 1
PAD = TOKENS + 1
TILE = PAD // 2
PD = PATCH * PATCH * CH
KP = PD // 128
HALF = HID // 2
REST = HID - 128
HPC = HEADS // 2
PPC = HPC // 2
STACK_DMAS = 3 * PPC
FCH = FFN // 128
GROUPS = HEADS // 4
GELU_PAIRS = FCH // 2
W1_PARTS = ((slice(0, 128), slice(0, 3 * FFN), slice(0, 3)), (slice(0, REST), slice(3 * FFN, 4 * FFN), slice(3, 4)))
KEYS0 = TILE + 1
PCOLS = PAD + KEYS0
MROW = 96
UP_BANK = (0, 1, 0, 1, 0, 1)
EPS = 1e-5
BIG = -1e30


class Image:

    def __init__(self, first, trip=None):
        self.first, self.trip = first, trip
        self.par = first % 2

    def count(self, per, more):
        c = per * self.first + more
        return c if self.trip is None else self.trip * (2 * per) + c

    def turns(self, per, more):
        c = per * (self.first // 2) + more
        return c if self.trip is None else self.trip * per + c

    def back(self, k):
        return Image(self.first - k, self.trip)

    def real(self):
        return self.trip is not None or 0 <= self.first < IMAGES

    def index(self):
        return self.first if self.trip is None else self.trip * 2 + self.first


class BankTurns:

    def __init__(self, pe):
        self.pe, self.last, self.trip = pe, {}, None

    def take(self, bank, image, read_done, per, more):
        if bank in self.last:
            sem, p, m, first = self.last[bank]
            self.pe.wait_ge(sem, Image(first, self.trip).count(p, m))
        self.last[bank] = (read_done, per, more, image.first)

    def leave(self, trips):
        self.last = {b: (s, p, m, f + 2 * (trips - 1)) for b, (s, p, m, f) in self.last.items()}
        self.trip = None


def run_turns(engine, turn, enter=None, leave=None):
    for n in range(-1, 3):
        turn(n, None)
    trips = (IMAGES - 6) // 2
    with engine.Fori(0, trips) as trip:
        if enter:
            enter(trip)
        turn(3, trip)
        turn(4, trip)
    if leave:
        leave(trips)
    for n in range(3 + 2 * trips, IMAGES + 2):
        turn(n, None)


def vit_tower(nc, x, tok_w, tok_bias, attn_w, proj_bias, cls, gate_w, w1, w2, b1, b2, out):
    ctx = ExitStack()
    with ctx:
        def sb(name, shape, dt=F32):
            return ctx.enter_context(nc.sbuf_tensor(name, shape, dt))

        def two(name, shape, dt=F32):
            return [sb(f"{name}{i}", shape, dt) for i in range(2)]

        def sem(name):
            return ctx.enter_context(nc.semaphore(name))

        w1_split = nc.dram_tensor("w1_split", [EXPERTS, 128, 4 * FFN], F32, kind="Internal").ap()

        w2_split = nc.dram_tensor("w2_split", [EXPERTS, 128, 2 * FCH * HID], F32, kind="Internal").ap()

        ident = sb("ident", [128, 128])
        ident_b = sb("ident_b", [TILE, TILE], BF16)
        causal0 = sb("causal0", [TILE, KEYS0], BF16)
        causal1 = sb("causal1", [TILE, KEYS0], BF16)
        head_rows = sb("head_rows", [MROW, HPC])
        even_odd = sb("even_odd", [MROW, 2])
        pick_max = sb("pick_max", [128, HPC])
        real_tok = sb("real_tok", [TILE, 2])
        ones_row = sb("ones_row", [1, TILE])
        minus_half = sb("minus_half", [TILE, 2])
        zero_col = sb("zero_col", [128, 1])
        tok_w_sb = sb("tok_w_sb", [128, KP, HID])
        tok_w_hi = sb("tok_w_hi", [128, KP, HID], F32R)
        tok_w_lo = sb("tok_w_lo", [128, KP, HID], F32R)
        tok_bias_sb = sb("tok_bias_sb", [TILE, 2, HID])
        proj_bias_sb = sb("proj_bias_sb", [TILE, HID])
        gate_w_sb = sb("gate_w_sb", [HALF, 2, EXPERTS])
        attn_w_sb = sb("attn_w_sb", [HALF, 2, 2, 4 * HID], F32R)

        x_sb = sb("x_sb", [128, KP, PAD])
        x_hi = sb("x_hi", [128, KP, PAD], F32R)
        x_lo = sb("x_lo", [128, KP, PAD], F32R)
        h_sb = sb("h_sb", [TILE, 2, HID])
        h_bias = two("h_bias", [TILE, 2, HID])
        xn = sb("xn", [TILE, 2, HID])
        stats = sb("stats", [TILE, 2, 6])
        mean_var = sb("mean_var", [TILE, 2, 2])
        var_eps = sb("var_eps", [TILE, 2])
        rstd = sb("rstd", [TILE, 2])
        xt_hi = sb("xt_hi", [HALF, 2, PAD], F32R)
        xt_lo = sb("xt_lo", [HALF, 2, PAD], F32R)
        k_hi = sb("k_hi", [HALF, 2, PAD], F32R)
        k_lo = sb("k_lo", [HALF, 2, PAD], F32R)
        q_hi = sb("q_hi", [HALF, 2, PAD], F32R)
        q_lo = sb("q_lo", [HALF, 2, PAD], F32R)
        q_st = two("q_st", [128, 2, PPC, PAD], F32R)
        k_st = two("k_st", [128, 2, HPC, PAD], F32R)
        k_pair = sb("k_pair", [MROW, 2, PPC, PAD])
        v_sb = two("v_sb", [TILE, 2, HEADS, 32])
        row_max = sb("row_max", [TILE, 2, HEADS])
        neg_max = sb("neg_max", [TILE, 2 * HEADS], F32R)
        max_cols = sb("max_cols", [TILE, 4, 128])
        pt_rows = sb("pt", [128, HEADS, PCOLS])
        pt = pt_rows[0:TILE]
        ot = sb("ot", [128, GROUPS, PAD])
        sum_inv = sb("sum_inv", [TILE, 2, HEADS])
        o_tok = sb("o_tok", [TILE, 2, HID])
        o_hi = sb("o_hi", [HALF, 2, PAD], F32R)
        o_lo = sb("o_lo", [HALF, 2, PAD], F32R)
        h2 = two("h2", [TILE, 2, HID])
        stats2 = sb("stats2", [TILE, 2, 6])
        mean_var2 = sb("mean_var2", [TILE, 2, 2])
        var_eps2 = sb("var_eps2", [TILE, 2])
        rstd2 = sb("rstd2", [TILE, 2])
        xn2 = sb("xn2", [TILE, 2, 256])
        xt2_hi = two("xt2_hi", [128, 2, PAD], F32R)
        xt2_lo = two("xt2_lo", [128, PAD], F32R)
        gate_sum = sb("gate_sum", [HALF, 2])
        logit = sb("logit", [1, EXPERTS])
        neg_top = sb("neg_top", [1, 1])
        gate_exp = sb("gate_exp", [1, EXPERTS])
        gate_den = sb("gate_den", [1, 1])
        gate_prob = sb("gate_prob", [1, 1])
        below_top = sb("below_top", [1, EXPERTS])
        second = sb("second", [1, 1])
        choice = sb("choice", [1, 1], I32)
        table_touch = sb("table_touch", [1, 2])
        weight = two("weight", [TILE, 1])
        w1_sb = two("w1_sb", [128, 4, FFN], F32R)
        w2_sb = two("w2_sb", [128, 2, FCH, HID], F32R)
        b1_sb = two("b1_sb", [128, FCH])
        b2_sb = two("b2_sb", [TILE, HID])
        act_sb = sb("act_sb", [128, FCH, PAD])
        act_hi = sb("act_hi", [128, FCH, PAD], F32R)
        act_lo = sb("act_lo", [128, FCH, PAD], F32R)
        y_sb = sb("y_sb", [TILE, 2, HID])
        out_sb = two("out_sb", [TILE, 2, HID])

        score = [ctx.enter_context(nc.psum_tensor(f"score{i}", [128, 2, 512], F32)) for i in range(2)]
        dense = [ctx.enter_context(nc.psum_tensor(f"dense{i}", [128, 512], F32)) for i in range(2)]
        turned = ctx.enter_context(nc.psum_tensor("turned", [128, 512], F32))
        mixed = ctx.enter_context(nc.psum_tensor("mixed", [128, 512], F32))

        s_small = sem("s_small")
        s_tok = sem("s_tok")
        table_loaded = sem("table_loaded")
        s_big = [sem(f"s_big{i}") for i in range(2)]
        s_zero = sem("s_zero")
        s_const = sem("s_const")
        s_mask = sem("s_mask")
        s_split = sem("s_split")
        s_saved = [sem(f"s_saved{i}") for i in range(2)]
        s_w2 = sem("s_w2")
        s_w2_split = sem("s_w2_split")
        s_w2_saved = [sem(f"s_w2_saved{i}") for i in range(2)]
        x_in = sem("x_in")
        x_hi_ready = sem("x_hi_ready")
        x_lo_ready = sem("x_lo_ready")
        s_tok_split = sem("s_tok_split")
        patch_mm = sem("patch_mm")
        h_ready = sem("h_ready")
        var_ready = sem("var_ready")
        rstd_ready = sem("rstd_ready")
        xn_ready = sem("xn_ready")
        hb_ready = sem("hb_ready")
        xt_mm = sem("xt_mm")
        xt_hi_ready = sem("xt_hi_ready")
        xt_lo_ready = sem("xt_lo_ready")
        qk_mm = sem("qk_mm")
        qk_hi_ready = sem("qk_hi_ready")
        qk_lo_ready = sem("qk_lo_ready")
        k_stacked = sem("k_stacked")
        q_stacked = [sem(f"q_stacked{i}") for i in range(2)]
        k_masked = sem("k_masked")
        v_mm = sem("v_mm")
        v_ready = sem("v_ready")
        smax_mm = sem("smax_mm")
        smax_done = sem("smax_done")
        negmax_ready = sem("negmax_ready")
        max_cols_ready = sem("max_cols_ready")
        max_mm = sem("max_mm")
        max_ready = sem("max_ready")
        score_mm = sem("score_mm")
        exp_done = sem("exp_done")
        causal_done = sem("causal_done")
        pv_mm = sem("pv_mm")
        ot_ready = sem("ot_ready")
        otr_mm = sem("otr_mm")
        inv_ready = sem("inv_ready")
        o_ready = sem("o_ready")
        o2_mm = sem("o2_mm")
        o_hi_ready = sem("o_hi_ready")
        o_lo_ready = sem("o_lo_ready")
        proj_mm = sem("proj_mm")
        h2_ready = sem("h2_ready")
        stats2_ready = sem("stats2_ready")
        var2_ready = sem("var2_ready")
        rstd2_ready = sem("rstd2_ready")
        xn2_ready = sem("xn2_ready")
        xt2_mm = sem("xt2_mm")
        xt2_hi_ready = sem("xt2_hi_ready")
        xt2_lo_ready = sem("xt2_lo_ready")
        gsum_mm = sem("gsum_mm")
        gsum_ready = sem("gsum_ready")
        logit_mm = sem("logit_mm")
        logit_ready = sem("logit_ready")
        top_ready = sem("top_ready")
        gexp_done = sem("gexp_done")
        prob_ready = sem("prob_ready")
        choice_ready = sem("choice_ready")
        choice_read = sem("choice_read")
        weight_mm = sem("weight_mm")
        weight_ready = sem("weight_ready")
        w1_in = [sem(f"w1_in{i}") for i in range(2)]
        w2_in = [sem(f"w2_in{i}") for i in range(2)]
        up_mm = sem("up_mm")
        gelu_done = sem("gelu_done")
        act_hi_ready = sem("act_hi_ready")
        act_lo0_ready = sem("act_lo0_ready")
        act_lo_ready = sem("act_lo_ready")
        down_mm = sem("down_mm")
        y_ready = sem("y_ready")
        out_ready = sem("out_ready")
        stored = [sem(f"stored{i}") for i in range(2)]
        dve_step = sem("dve_step")
        unused = sem("unused")

        def score_slot(image, k):
            return (11 * image.par + k) % 2

        stage = pt_rows[:].rearrange("p h c -> p (h c)")

        def staged(i, rows=128):
            return stage[0:rows, i * 2 * FFN:(i + 1) * 2 * FFN].rearrange("p (c n) -> p c n", c=2)

        staged_w2 = act_sb[:].rearrange("p m t -> p (m t)")[:, 0:FCH * HID]

        def stand_alone(engine):
            engine.sem_inc(unused, 1)

        block = ctx.enter_context(nc.Block())

        @block.sync
        def _(sp):
            def stage_w1(e):
                i = (e + 1) % 2
                sp.dma_start(staged(i), w1[e]).then_inc(s_big[i], 16)

            def save_w1(e):
                sp.wait_ge(s_split, 2 + 3 * (e + 1))
                for rows, cols, blocks in W1_PARTS:
                    sp.dma_start(w1_split[e, rows, cols], w1_sb[e % 2][rows, blocks].bitcast(F32).rearrange(
                        "p b n -> p (b n)")).then_inc(s_saved[e % 2], 16)

            def save_w2(e):
                sp.wait_ge(s_w2_split, 2 * (e + 1))
                if e + 1 < EXPERTS:
                    sp.dma_start(staged_w2, w2[e + 1]).then_inc(s_w2, 16)
                sp.dma_start(w2_split[e], w2_sb[e % 2][:].bitcast(F32).rearrange("p s m n -> p (s m n)")).then_inc(s_w2_saved[e % 2], 16)

            def load_x(e):
                sp.wait_ge(x_lo_ready, e.back(1).count(2, 2))
                sp.dma_start(x_sb[:], x[e.index()]).then_inc(x_in, 16)

            def load_expert(c):
                sp.wait_ge(choice_ready, c.count(1, 1))
                stand_alone(sp)
                e = sp.value_load(choice[0:1, 0:1], min_val=0, max_val=EXPERTS - 1)
                if c.trip is not None or c.first >= 2:
                    sp.wait_ge(out_ready, c.back(2).count(2, 2))
                for rows, cols, blocks in W1_PARTS:
                    sp.dma_start(w1_sb[c.par][rows, blocks].bitcast(F32).rearrange("p b n -> p (b n)"),
                                 w1_split[e, rows, cols]).then_inc(w1_in[c.par], 16)
                sp.dma_start(b1_sb[c.par][:], b1[e]).then_inc(w1_in[c.par], 16)
                sp.dma_start(w2_sb[c.par][:].bitcast(F32).rearrange("p s m n -> p (s m n)"), w2_split[e]).then_inc(w2_in[c.par], 16)
                sp.dma_start(b2_sb[c.par][:], b2[e].partition_broadcast(TILE)).then_inc(w2_in[c.par], 16)
                sp.sem_inc(choice_read, 1)

            def stack(a, half):
                sp.wait_ge(qk_lo_ready, a.count(2, half + 1))
                if half == 0 and (a.trip is not None or a.first >= 1):
                    stand_alone(sp)
                    sp.wait_ge(k_masked, a.back(1).count(2, 2))
                if half == 1 and (a.trip is not None or a.first >= 2):
                    stand_alone(sp)
                    sp.wait_ge(score_mm, a.back(2).count(6, 6))
                stand_alone(sp)
                dst, blocks = ((k_pair, (k_hi, k_hi, k_lo)), (q_st[a.par], (q_hi, q_lo, q_hi)))[half]
                done = (k_stacked, q_stacked[a.par])[half]
                for i in range(PPC):
                    for block, src in enumerate(blocks):
                        to = dst[32 * block:32 * block + 32, :, i, :]
                        sp.dma_start(to if half == 0 else to.bitcast(F32),
                                     src[32 * i:32 * i + 32, :, :].bitcast(F32)).then_inc(done, 16)

            def store(d):
                for j in range(2):
                    sp.wait_ge(out_ready, d.count(2, j + 1))
                    rows = TILE - j
                    sp.dma_start(out[d.index(), j * TILE:j * TILE + rows, :],
                                 out_sb[d.par][0:rows, j, :]).then_inc(stored[d.par], 16)

            sp.dma_start(tok_w_sb[:], tok_w).then_inc(s_tok, 16)
            sp.dma_start(x_sb[:], x[0]).then_inc(x_in, 16)
            sp.dma_start(staged(0, HALF), attn_w.rearrange("(c p) n -> p c n", c=2)).then_inc(s_big[0], 16)
            sp.dma_start(tok_bias_sb[:, 0, :], tok_bias.partition_broadcast(TILE)).then_inc(s_small, 16)
            sp.dma_start(tok_bias_sb[:, 1, :], tok_bias.partition_broadcast(TILE)).then_inc(s_small, 16)
            sp.dma_start(proj_bias_sb[:], proj_bias.partition_broadcast(TILE)).then_inc(s_small, 16)
            sp.dma_start(gate_w_sb[:], gate_w).then_inc(s_small, 16)
            stage_w1(0)
            sp.dma_start(staged_w2, w2[0]).then_inc(s_w2, 16)
            sp.wait_ge(s_small, 64)
            sp.dma_start(tok_bias_sb[0:1, 0, :], cls).then_inc(s_small, 16)
            load_x(Image(1))
            sp.wait_ge(s_split, 2)
            stage_w1(1)
            sp.wait_ge(s_split, 5)
            stage_w1(2)
            save_w1(0)
            save_w1(1)
            save_w2(0)
            save_w1(2)
            stack(Image(0), 0)
            save_w2(1)
            stack(Image(0), 1)
            save_w2(2)
            sp.wait_ge(s_saved[0], 64)
            sp.wait_ge(s_saved[1], 32)
            sp.wait_ge(s_w2_saved[0], 32)
            sp.wait_ge(s_w2_saved[1], 16)

            def turn(n, trip):
                f, a, c, d = (Image(n + k, trip) for k in (3, 1, -1, -2))
                if a.real() and n >= 0:
                    stack(a, 0)
                    stack(a, 1)
                if c.real():
                    load_expert(c)
                if f.real():
                    load_x(f)
                if d.real():
                    store(d)

            run_turns(sp, turn)
            for s in stored:
                sp.wait_ge(s, 16 * IMAGES)

        @block.gpsimd
        def _(pool):
            g = nc.gpsimd
            g.memset(ident[:], 0.0).then_inc(s_zero, 1)
            g.memset(ident_b[:], 0.0).then_inc(s_zero, 1)
            g.memset(causal0[:], 0.0).then_inc(s_zero, 1)
            g.memset(causal1[:], 0.0).then_inc(s_zero, 1)
            g.memset(head_rows[:], 1.0).then_inc(s_zero, 1)
            g.memset(pick_max[:], 0.0).then_inc(s_zero, 1)
            g.memset(real_tok[:], 1.0).then_inc(s_zero, 1)
            g.memset(ones_row[:], 1.0).then_inc(s_const, 1)
            g.memset(minus_half[:], -0.5).then_inc(s_const, 1)
            g.memset(max_cols[:], 0.0).then_inc(s_const, 1)
            g.memset(zero_col[:], 0.0).then_inc(s_zero, 1)
            for i in range(2):
                g.memset(v_sb[i][:], 0.0).then_inc(s_zero, 1)
            pool.wait_ge(s_zero, 10)
            g.affine_select(out=ident[:], in_=ident[:], compare_op=ALU.not_equal, fill=1.0, base=0,
                            pattern=[[-1, 128]], channel_multiplier=1).then_inc(s_const, 1)
            g.affine_select(out=ident_b[:], in_=ident_b[:], compare_op=ALU.not_equal, fill=1.0, base=0,
                            pattern=[[-1, TILE]], channel_multiplier=1).then_inc(s_const, 1)
            g.affine_select(out=causal0[:], in_=causal0[:], compare_op=ALU.is_ge, fill=BIG, base=0,
                            pattern=[[-1, KEYS0]], channel_multiplier=1).then_inc(s_const, 1)
            g.affine_select(out=causal1[:], in_=causal1[:], compare_op=ALU.is_ge, fill=BIG, base=1,
                            pattern=[[-1, KEYS0]], channel_multiplier=1).then_inc(s_const, 1)
            g.affine_select(out=real_tok[:], in_=real_tok[:], compare_op=ALU.not_equal, fill=0.0,
                            base=-(TILE - 1 + 1), pattern=[[1, 2]], channel_multiplier=1).then_inc(s_const, 1)
            g.affine_select(out=head_rows[:], in_=head_rows[:], compare_op=ALU.is_ge, fill=0.0, base=0,
                            pattern=[[-HD, HPC]], channel_multiplier=1).then_inc(s_zero, 1)
            pool.wait_ge(s_zero, 11)
            g.affine_select(out=head_rows[:], in_=head_rows[:], compare_op=ALU.is_ge, fill=0.0, base=HD - 1,
                            pattern=[[HD, HPC]], channel_multiplier=-1).then_inc(s_const, 1)
            for part in range(2):
                g.affine_select(out=pick_max[:], in_=pick_max[:], compare_op=ALU.not_equal,
                                fill=1.0, base=-MROW - HPC * part, pattern=[[-1, HPC]],
                                channel_multiplier=1).then_inc(s_zero, 1)
                pool.wait_ge(s_zero, 12 + part)
            for i in range(2):
                g.memset(v_sb[i][:, :, :, HD:HD + 1], 1.0).then_inc(s_const, 1)

            def act_low_first(d):
                pool.wait_ge(act_hi_ready, d.count(GELU_PAIRS, 1))
                g.tensor_tensor(act_lo[:, 0:2, :], act_sb[:, 0:2, :], act_hi[:, 0:2, :].bitcast(F32),
                                ALU.subtract).then_inc(act_lo0_ready, 1)

            def rstd_of(image, ready, src, done, dst):
                pool.wait_ge(ready, image.count(1, 1))
                g.tensor_tensor(dst[:], src[:], minus_half[:], ALU.pow).then_inc(done, 1)

            def residual_bias(a):
                pool.wait_ge(h_ready, a.count(2, 2))
                if a.trip is not None or a.first >= 2:
                    pool.wait_ge(h2_ready, a.back(2).count(1, 1))
                g.tensor_tensor(h_bias[a.par][:], h_sb[:],
                                proj_bias_sb[:].unsqueeze(1).to_broadcast([TILE, 2, HID]), ALU.add).then_inc(hb_ready, 1)

            def mask_keys(a, z):
                pool.wait_ge(k_stacked, a.count(16 * STACK_DMAS, 16 * STACK_DMAS))
                if z == 0 and (a.trip is not None or a.first >= 2):
                    pool.wait_ge(score_mm, a.back(2).count(6, 6))
                stand_alone(pool)
                g.tensor_scalar(k_st[a.par][0:MROW].rearrange("p c (i z) t -> p c i z t", z=2)[:, :, :, z, :],
                                k_pair[:], even_odd[:, z:z + 1], 1.0, ALU.mult, ALU.mult).then_inc(k_masked, 1)

            def hide_future(b, s):
                pool.wait_ge(exp_done, b.count(6, s + 1))
                stand_alone(pool)
                v = pt[:, 2 * s:2 * s + 2, 0:2 * KEYS0].rearrange("p h (r q) -> p h r q", r=2)
                g.affine_select(out=v, in_=v, compare_op=ALU.is_ge, fill=0.0, base=-1,
                                pattern=[[0, 2], [1, 2], [1, KEYS0]], channel_multiplier=-1).then_inc(causal_done, 1)

            pool.wait_ge(s_small, 80)
            pool.wait_ge(s_const, 11)
            pool.wait_ge(s_mask, 1)

            def turn(n, trip):
                a, b, c, d = (Image(n + k, trip) for k in (1, 0, -1, -2))
                if c.real():
                    hide_future(c, 5)
                if a.real():
                    rstd_of(a, var_ready, var_eps, rstd_ready, rstd)
                    residual_bias(a)
                if c.real():
                    rstd_of(c, var2_ready, var_eps2, rstd2_ready, rstd2)
                if d.real():
                    act_low_first(d)
                if a.real():
                    mask_keys(a, 0)
                if b.real():
                    hide_future(b, 0)
                    hide_future(b, 1)
                if a.real():
                    mask_keys(a, 1)
                if b.real():
                    for s in range(2, 5):
                        hide_future(b, s)

            run_turns(pool, turn)

        @block.scalar
        def _(act):
            act.wait_ge(s_zero, 13)
            for w in w1_sb:
                nc.scalar.activation(w[REST:128, 3, :], zero_col[REST:128, :].to_broadcast([128 - REST, FFN]),
                                     ACT.Copy).then_inc(s_const, 1)
            for i in range(2):
                for c in range(2):
                    nc.scalar.activation(k_st[i][MROW:128, c, :, :],
                                         pick_max[MROW:128, :].unsqueeze(2).to_broadcast([128 - MROW, HPC, PAD]),
                                         ACT.Copy).then_inc(s_const, 1)

            def hi(image, dst, src, ready, per, k, done):
                act.wait_ge(ready, image.count(per, k))
                nc.scalar.activation(dst, src, ACT.Copy).then_inc(done, 1)

            def both(bank, rows=HALF):
                return bank[0:rows, 0:2 * PAD].rearrange("p (c t) -> p c t", c=2)

            def x_high(e, t):
                act.wait_ge(x_in, e.count(16, 16))
                if e.trip is not None or e.first >= 1:
                    act.wait_ge(patch_mm, e.back(1).count(2, t + 1))
                tok = slice(t * TILE, (t + 1) * TILE)
                nc.scalar.activation(x_hi[:, :, tok], x_sb[:, :, tok], ACT.Copy).then_inc(x_hi_ready, 1)

            def xt(a):
                if a.trip is not None or a.first >= 1:
                    act.wait_ge(v_mm, a.back(1).count(1, 1))
                hi(a, xt_hi[:], both(turned), xt_mm, 1, 1, xt_hi_ready)

            def qk(a, u):
                if a.trip is not None or a.first >= 1:
                    if u == 0:
                        act.wait_ge(k_stacked, a.back(1).count(16 * STACK_DMAS, 16 * STACK_DMAS))
                    else:
                        act.wait_ge(q_stacked[1 - a.par], a.back(1).turns(16 * STACK_DMAS, 16 * STACK_DMAS))
                hi(a, (k_hi, q_hi)[u][:], both((dense[0], mixed)[u]), qk_mm, 2, u + 1, qk_hi_ready)

            def values(a):
                act.wait_ge(v_mm, a.count(1, 1))
                if a.trip is not None or a.first >= 2:
                    act.wait_ge(pv_mm, a.back(2).count(GROUPS, GROUPS))
                nc.scalar.activation(v_sb[a.par][:, :, :, 0:HD],
                                     turned[0:TILE, 0:2 * HID].rearrange("p (t h d) -> p t h d", t=2, h=HEADS),
                                     ACT.Copy).then_inc(v_ready, 1)

            def max_rows(b):
                act.wait_ge(max_mm, b.count(1, 1))
                rows = mixed[MROW:128, 0:2 * PAD].rearrange("p (c t) -> p c t", c=2)
                nc.scalar.activation(q_st[b.par][MROW:128, :, :, :],
                                     rows.unsqueeze(2).to_broadcast([128 - MROW, 2, PPC, PAD]),
                                     ACT.Copy).then_inc(max_ready, 1)

            def exps(b, s):
                act.wait_ge(score_mm, b.count(6, s + 1))
                if s == 0 and b.trip is None and b.first == 0:
                    act.wait_ge(s_split, 2 + 3 * EXPERTS)
                if s % 2 == 0 and (b.trip is not None or b.first >= 1):
                    act.wait_ge(pv_mm, b.back(1).count(GROUPS, s // 2 + 1))
                nc.scalar.activation(pt[:, 2 * s:2 * s + 2, :],
                                     score[score_slot(b, 5 + s)][0:TILE, :, 2 * PAD - PCOLS:2 * PAD],
                                     ACT.Exp, scale=HD ** -0.5).then_inc(exp_done, 1)

            def mixed_out(b, g):
                act.wait_ge(pv_mm, b.count(GROUPS, g + 1))
                if g == 0 and (b.trip is not None or b.first >= 1):
                    act.wait_ge(otr_mm, b.back(1).count(2, 2))
                nc.scalar.activation(ot[:, g, :], mixed[:, 0:PAD], ACT.Copy).then_inc(ot_ready, 1)

            def load_table(image, k, function):
                if image.trip is not None or image.first >= 1:
                    act.wait_ge(table_loaded, image.back(1).count(2, k + 1))
                nc.scalar.activation(table_touch[:, k:k + 1], minus_half[0:1, 0:1], function).then_inc(table_loaded, 1)

            def o_high(c):
                if c.trip is not None or c.first >= 1:
                    act.wait_ge(proj_mm, c.back(1).count(1, 1))
                hi(c, o_hi[:], both(mixed), o2_mm, 1, 1, o_hi_ready)

            def xt2(c):
                if c.trip is not None or c.first >= 2:
                    act.wait_ge(up_mm, c.back(2).count(FCH, FCH))
                hi(c, xt2_hi[c.par][:], both(mixed, 128), xt2_mm, 1, 1, xt2_hi_ready)

            def gate_exps(c):
                act.wait_ge(top_ready, c.count(1, 1))
                nc.scalar.activation(gate_exp[:], logit[:], ACT.Exp, bias=neg_top[:],
                                     accum_out=gate_den[:]).then_inc(gexp_done, 1)

            def gelu(d, m):
                act.wait_ge(up_mm, d.count(FCH, m + 1))
                if m == 0:
                    act.wait_ge(w1_in[d.par], d.turns(48, 48))
                    if d.trip is None and d.first == 0:
                        act.wait_ge(s_w2_split, 2 * EXPERTS)
                if m == 0 and (d.trip is not None or d.first >= 1):
                    act.wait_ge(act_lo0_ready, d.back(1).count(1, 1))
                    act.wait_ge(act_lo_ready, d.back(1).count(GELU_PAIRS - 1, GELU_PAIRS - 1))
                nc.scalar.activation(act_sb[:, m, :], dense[UP_BANK[m]][:, 0:PAD], ACT.Gelu,
                                     bias=b1_sb[d.par][:, m:m + 1]).then_inc(gelu_done, 1)

            def act_high(d, i):
                act.wait_ge(gelu_done, d.count(FCH, 2 * i + 2))
                if i == 0 and (d.trip is not None or d.first >= 1):
                    act.wait_ge(down_mm, d.back(1).count(2, 2))
                nc.scalar.activation(act_hi[:, 2 * i:2 * i + 2, :], act_sb[:, 2 * i:2 * i + 2, :],
                                     ACT.Copy).then_inc(act_hi_ready, 1)

            def turn(n, trip):
                e, a, b, c, d = (Image(n + k, trip) for k in (2, 1, 0, -1, -2))
                E, A, B, C, D = e.real(), a.real(), b.real(), c.real(), d.real()
                if C:
                    exps(c, 5)
                    mixed_out(c, 1)
                    mixed_out(c, 2)
                if D:
                    load_table(d, 0, ACT.Gelu)
                    gelu(d, 0)
                if A:
                    xt(a)
                if C:
                    o_high(c)
                if D:
                    gelu(d, 1)
                if A:
                    qk(a, 0)
                if E:
                    x_high(e, 0), x_high(e, 1)
                if A:
                    qk(a, 1)
                    values(a)
                if D:
                    gelu(d, 2), gelu(d, 3)
                    act_high(d, 0)
                    gelu(d, 4)
                    act_high(d, 1)
                    gelu(d, 5)
                    act_high(d, 2)
                if B:
                    max_rows(b)
                if D:
                    load_table(d, 1, ACT.Exp)
                if B:
                    exps(b, 0), exps(b, 1)
                if C:
                    gate_exps(c)
                    xt2(c)
                if B:
                    exps(b, 2), exps(b, 3)
                    mixed_out(b, 0)
                    exps(b, 4)

            x_high(Image(0), 0)
            x_high(Image(0), 1)
            run_turns(act, turn)

        @block.vector
        def _(dve):
            v = nc.vector
            dve.wait_ge(s_tok, 16)
            v.tensor_copy(tok_w_hi[:], tok_w_sb[:]).then_inc(s_tok_split, 1)
            dve.wait_ge(s_tok_split, 1)
            v.tensor_tensor(tok_w_lo[:], tok_w_sb[:], tok_w_hi[:].bitcast(F32), ALU.subtract).then_inc(s_tok_split, 1)
            def split_attn():
                dve.wait_ge(s_big[0], 16)
                v.tensor_copy(attn_w_sb[:, :, 0, :], staged(0, HALF)).then_inc(s_split, 1)
                dve.wait_ge(s_split, 1)
                v.tensor_tensor(attn_w_sb[:, :, 1, :], staged(0, HALF), attn_w_sb[:, :, 0, :].bitcast(F32),
                                ALU.subtract).then_inc(s_split, 1)

            def split_w1(e):
                half, dst = (e + 1) % 2, w1_sb[e % 2]
                dve.wait_ge(s_big[half], 16 * ((e + 1) // 2 + 1))
                if e == 2:
                    dve.wait_ge(s_saved[0], 32)
                v.tensor_copy(dst[:].rearrange("p (b s) n -> p b s n", s=2)[:, :, 0, :], staged(half)).then_inc(s_split, 1)
                dve.wait_ge(s_split, 2 + 3 * e + 1)
                v.tensor_tensor(dst[:, 1, :], staged(half)[:, 0, :], dst[:, 0, :].bitcast(F32),
                                ALU.subtract).then_inc(s_split, 1)
                v.tensor_tensor(dst[0:REST, 3, :], staged(half)[0:REST, 1, :], dst[0:REST, 2, :].bitcast(F32),
                                ALU.subtract).then_inc(s_split, 1)

            def split_w2(e):
                dve.wait_ge(s_w2, 16 * (e + 1))
                if e == 2:
                    dve.wait_ge(s_w2_saved[0], 16)
                cut = staged_w2.rearrange("p (m n) -> p m n", m=FCH)
                v.tensor_copy(w2_sb[e % 2][:, 0], cut).then_inc(s_w2_split, 1)
                dve.wait_ge(s_w2_split, 2 * e + 1)
                v.tensor_tensor(w2_sb[e % 2][:, 1], cut, w2_sb[e % 2][:, 0].bitcast(F32),
                                ALU.subtract).then_inc(s_w2_split, 1)

            dve.wait_ge(s_const, 17)
            dve.wait_ge(s_small, 80)
            v.reduce_sum(even_odd[:], head_rows[:].rearrange("p (i z) -> p z i", z=2), AX_X).then_inc(s_mask, 1)

            def low(image, dst, src, high, ready, per, k, done):
                dve.wait_ge(ready, image.count(per, k))
                v.tensor_tensor(dst, src, high.bitcast(F32), ALU.subtract).then_inc(done, 1)

            def both(bank, rows=HALF):
                return bank[0:rows, 0:2 * PAD].rearrange("p (c t) -> p c t", c=2)

            def stacked_low(image, dst, bank, high, ready, done):
                dve.wait_ge(ready, image.count(1, 1))
                v.tensor_tensor(dst[:], bank[:, 0:PAD], high[:, 0, :].bitcast(F32), ALU.subtract).then_inc(done, 1)
                v.tensor_tensor(high[REST:128, 1, :], bank[REST:128, PAD:2 * PAD], high[REST:128, 1, :].bitcast(F32),
                                ALU.subtract).then_inc(done, 1)

            class Steps:
                per_turn = 10

                def __init__(self):
                    self.n, self.trip = 0, None

                def link(self, instruction):
                    instruction.then_inc(dve_step, 1)
                    self.n += 1
                    dve.wait_ge(dve_step, self.n if self.trip is None else self.trip * (2 * self.per_turn) + self.n)

            def x_low(e, t):
                tok = slice(t * TILE, (t + 1) * TILE)
                low(e, x_lo[:, :, tok], x_sb[:, :, tok], x_hi[:, :, tok], x_hi_ready, 2, t + 1, x_lo_ready)

            def act_low(d, i):
                pair = slice(2 * i, 2 * i + 2)
                dve.wait_ge(act_hi_ready, d.count(GELU_PAIRS, i + 1))
                v.tensor_tensor(act_lo[:, pair, :], act_sb[:, pair, :], act_hi[:, pair, :].bitcast(F32),
                                ALU.subtract).then_inc(act_lo_ready, 1)

            steps = Steps()
            link = steps.link

            def block_max(b, k):
                dve.wait_ge(smax_mm, b.count(5, k + 1))
                if k == 0 and (b.trip is not None or b.first >= 1):
                    dve.wait_ge(max_cols_ready, b.back(1).count(1, 1))
                slot = score[score_slot(b, k)]
                if k < 2:
                    heads = 4 - 2 * k
                    v.reduce_max(row_max[:, 0, 8 * k:8 * k + 2 * heads].rearrange("p (z h) -> p z h", z=2),
                                 slot[0:TILE, :, 0:heads * KEYS0].rearrange("p z (h k) -> p z h k", h=heads),
                                 AX_X).then_inc(smax_done, 1)
                else:
                    h = 4 * (k - 2)
                    v.reduce_max(row_max[:, 1, h:h + 4].rearrange("p (z h) -> p z h", z=2),
                                 slot[0:TILE, :, 0:2 * PAD].rearrange("p z (h k) -> p z h k", h=2),
                                 AX_X).then_inc(smax_done, 1)

            def normalise(c, j):
                bank = (turned, mixed)[j]
                view = bank[0:TILE, 0:HEADS * 32].rearrange("p (h e) -> p h e", h=HEADS)
                dve.wait_ge(otr_mm, c.count(2, j + 1))
                if j == 0 and (c.trip is not None or c.first >= 1):
                    dve.wait_ge(o2_mm, c.back(1).count(1, 1))
                v.reciprocal(sum_inv[:, j, :], view[:, :, HD]).then_inc(inv_ready, 1)
                dve.wait_ge(inv_ready, c.count(2, j + 1))
                v.tensor_tensor(o_tok[:, j, :].rearrange("p (h e) -> p h e", h=HEADS), view[:, :, 0:HD],
                                sum_inv[:, j, :].unsqueeze(2).to_broadcast([TILE, HEADS, HD]),
                                ALU.mult).then_inc(o_ready, 1)

            def twice(image, dst, done):
                dve.wait_ge(done, image.count(3, 2))
                v.tensor_copy(dst[:, :, HID:256], dst[:, :, 128:HID]).then_inc(done, 1)

            def embed(a, t):
                dve.wait_ge(patch_mm, a.count(2, t + 1))
                if t == 0 and (a.trip is not None or a.first >= 1):
                    dve.wait_ge(hb_ready, a.back(1).count(1, 1))
                v.tensor_tensor(h_sb[:, t, :], dense[t][0:TILE, 0:HID], tok_bias_sb[:, t, :], ALU.add).then_inc(h_ready, 1)
                dve.wait_ge(h_ready, a.count(2, t + 1))
                link(v.bn_stats(stats[:, t, :], h_sb[:, t, :]))
                stand_alone(dve)
                link(v.bn_aggr(mean_var[:, t, :], stats[:, t, :]))

            def residual(c):
                dve.wait_ge(proj_mm, c.count(1, 1))
                dve.wait_ge(hb_ready, c.count(1, 1))
                v.tensor_tensor(h2[c.par][:], dense[1][0:TILE, 0:2 * HID].rearrange("p (j n) -> p j n", j=2),
                                h_bias[c.par][:], ALU.add).then_inc(h2_ready, 1)
                dve.wait_ge(h2_ready, c.count(1, 1))
                for j in range(2):
                    v.bn_stats(stats2[:, j, :], h2[c.par][:, j, :]).then_inc(stats2_ready, 1)
                for j in range(2):
                    dve.wait_ge(stats2_ready, c.count(2, j + 1))
                    stand_alone(dve)
                    link(v.bn_aggr(mean_var2[:, j, :], stats2[:, j, :]))

            def variance(dst, mv, done):
                v.tensor_scalar(dst[:], mv[:, :, 1], EPS, None, ALU.add).then_inc(done, 1)

            def layer_norm(image, dst, src, mv, rs, ready, done, used):
                dve.wait_ge(ready, image.count(1, 1))
                if image.trip is not None or image.first >= 1:
                    sem_used, per = used
                    dve.wait_ge(sem_used, image.back(1).count(per, per))
                for t in range(2):
                    v.tensor_scalar(dst[:, t, 0:HID], src[:, t, :], mv[:, t, 0:1], rs[:, t:t + 1],
                                    ALU.subtract, ALU.mult).then_inc(done, 1)

            def spread_max(b):
                m = row_max[:].rearrange("p j h -> p (j h)")
                dve.wait_ge(smax_done, b.count(5, 5))
                if b.trip is not None or b.first >= 1:
                    dve.wait_ge(max_mm, b.back(1).count(1, 1))
                v.tensor_scalar(neg_max[:], m, -1.0, None, ALU.mult).then_inc(negmax_ready, 1)
                dve.wait_ge(negmax_ready, b.count(1, 1))
                grouped = "p (g h) -> p g h"
                link(v.tensor_copy(max_cols[:, :, MROW:MROW + HPC],
                                   neg_max[:].bitcast(F32).rearrange(grouped, g=4)))
                v.scalar_tensor_tensor(out=max_cols[:, :, MROW + HPC:MROW + 2 * HPC],
                                       in0=m.rearrange(grouped, g=4), scalar=-1.0,
                                       in1=neg_max[:].bitcast(F32).rearrange(grouped, g=4),
                                       op0=ALU.mult, op1=ALU.subtract).then_inc(max_cols_ready, 1)

            def gate_sums(c):
                dve.wait_ge(gsum_mm, c.count(1, 1))
                v.tensor_copy(gate_sum[:], turned[0:HALF, 0:2]).then_inc(gsum_ready, 1)

            def gate(c):
                dve.wait_ge(logit_mm, c.count(1, 1))
                if c.trip is not None or c.first >= 1:
                    dve.wait_ge(gexp_done, c.back(1).count(1, 1))
                v.tensor_scalar(logit[:], turned[0:1, 0:EXPERTS], 1.0 / TOKENS, None, ALU.mult).then_inc(logit_ready, 1)
                dve.wait_ge(logit_ready, c.count(1, 1))
                link(v.reduce_max(second[:], logit[:], AX_X))
                v.tensor_scalar(neg_top[:], second[:], -1.0, None, ALU.mult).then_inc(top_ready, 1)
                link(v.tensor_scalar(below_top[:], logit[:], second[:], None, ALU.is_lt))
                link(v.tensor_scalar(second[:], below_top[:, 1:2], 1.0, None, ALU.add))
                if c.trip is not None or c.first >= 1:
                    dve.wait_ge(choice_read, c.back(1).count(1, 1))
                v.tensor_tensor(choice[:], second[:], below_top[:, 0:1], ALU.mult).then_inc(choice_ready, 1)

            def gate_weight(c):
                dve.wait_ge(gexp_done, c.count(1, 1))
                v.reciprocal(gate_prob[:], gate_den[:]).then_inc(prob_ready, 1)

            def spread_weight(c):
                dve.wait_ge(weight_mm, c.count(1, 1))
                v.tensor_copy(weight[c.par][:], turned[0:TILE, 0:1]).then_inc(weight_ready, 1)

            def finish(d, j):
                dve.wait_ge(down_mm, d.count(2, j + 1))
                if j == 0:
                    dve.wait_ge(w2_in[d.par], d.turns(32, 32))
                    dve.wait_ge(weight_ready, d.count(1, 1))
                    if d.trip is not None or d.first >= 1:
                        dve.wait_ge(out_ready, d.back(1).count(2, 2))
                    if d.trip is not None or d.first >= 2:
                        dve.wait_ge(stored[d.par], d.turns(32, 0))
                v.tensor_tensor(y_sb[:, j, :], dense[j][0:TILE, 0:HID], b2_sb[d.par][:], ALU.add).then_inc(y_ready, 1)
                dve.wait_ge(y_ready, d.count(2, j + 1))
                v.scalar_tensor_tensor(out=out_sb[d.par][:, j, :], in0=y_sb[:, j, :], scalar=weight[d.par][:, 0:1],
                                       in1=h2[d.par][:, j, :], op0=ALU.mult, op1=ALU.add).then_inc(out_ready, 1)

            def qk_low(a, u):
                low(a, (k_lo, q_lo)[u][:], both((dense[0], mixed)[u]), (k_hi, q_hi)[u][:], qk_hi_ready, 2, u + 1, qk_lo_ready)

            def turn(n, trip):
                e, a, b, c, d = (Image(n + k, trip) for k in (2, 1, 0, -1, -2))
                E, A, B, C, D = e.real(), a.real(), b.real(), c.real(), d.real()
                if A:
                    embed(a, 0)
                    embed(a, 1)
                    variance(var_eps, mean_var, var_ready)
                if n == -1:
                    split_w1(1)
                if D:
                    spread_weight(d)
                if B:
                    block_max(b, 0)
                if A:
                    layer_norm(a, xn, h_sb, mean_var, rstd, rstd_ready, xn_ready, (xt_mm, 1))
                if n == -1:
                    split_w2(0)
                if C:
                    normalise(c, 0), normalise(c, 1)
                if B:
                    block_max(b, 1)
                if A:
                    low(a, xt_lo[:], both(turned), xt_hi[:], xt_hi_ready, 1, 1, xt_lo_ready)
                if n == -1:
                    split_w1(2)
                if B:
                    block_max(b, 2)
                if C:
                    low(c, o_lo[:], both(mixed), o_hi[:], o_hi_ready, 1, 1, o_lo_ready)
                if A:
                    qk_low(a, 0)
                if n == -1:
                    split_w2(1)
                if B:
                    block_max(b, 3)
                if C:
                    residual(c)
                    variance(var_eps2, mean_var2, var2_ready)
                if A:
                    qk_low(a, 1)
                if n == -1:
                    split_w2(2)
                if B:
                    block_max(b, 4)
                    spread_max(b)
                if C:
                    layer_norm(c, xn2, h2[c.par], mean_var2, rstd2, rstd2_ready, xn2_ready, (xt2_mm, 1))
                if D:
                    act_low(d, 1)
                if C:
                    gate_sums(c)
                    twice(c, xn2, xn2_ready)
                if D:
                    act_low(d, 2)
                if E:
                    x_low(e, 0)
                if C:
                    gate(c)
                if D:
                    finish(d, 0)
                if C:
                    stacked_low(c, xt2_lo[c.par], mixed, xt2_hi[c.par], xt2_hi_ready, xt2_lo_ready)
                    gate_weight(c)
                if D:
                    finish(d, 1)
                if E:
                    x_low(e, 1)

            x_low(Image(0), 0)
            x_low(Image(0), 1)
            split_attn()
            split_w1(0)
            start = []

            def enter(trip):
                start.append(steps.n)
                steps.trip = trip

            def leave(trips):
                steps.trip = None
                assert steps.n - start[0] == 2 * steps.per_turn, (steps.n - start[0]) / 2
                steps.n += 2 * steps.per_turn * (trips - 1)

            run_turns(dve, turn, enter, leave)

        @block.tensor
        def _(pe):
            mm = nc.tensor.matmul
            turns = BankTurns(pe)
            pe.wait_ge(s_small, 80)
            pe.wait_ge(s_tok_split, 2)
            pe.wait_ge(s_const, 17)
            pe.wait_ge(s_split, 2)

            def three(dst, pairs):
                ops = [p for lh, ll, rh, rl in pairs for p in ((lh, rh), (lh, rl), (ll, rh))]
                for i, (l, r) in enumerate(ops):
                    last = mm(dst, l, r, start=(i == 0), stop=(i == len(ops) - 1))
                return last

            def stacked_q(b, h, rows):
                return q_st[b.par][rows, h // HPC, h % HPC // 2, :]

            def score_max(b, k):
                slot = score_slot(b, k)
                turns.take(("score", slot), b, smax_done, 5, k + 1)
                if k == 0:
                    pe.wait_ge(q_stacked[b.par], b.turns(16 * STACK_DMAS, 16 * STACK_DMAS))
                    pe.wait_ge(k_masked, b.count(2, 2))
                for z in range(2):
                    if k < 2:
                        heads, keys, t, hidden, first = 4 - 2 * k, KEYS0, 0, causal0, 0
                        h = 8 * k + heads * z
                    else:
                        heads, keys, t, hidden, first = 2, PAD, 1, causal1, PAD - KEYS0
                        h = 4 * (k - 2) + 2 * z
                    dst = score[slot][0:TILE, z, 0:heads * keys].rearrange("p (h k) -> p h k", h=heads)
                    for i in range(0, heads, 2):
                        mm(dst[:, i:i + 2], stacked_q(b, h + i, slice(0, MROW))[:, t * TILE:(t + 1) * TILE],
                           k_st[b.par][0:MROW, (h + i) // HPC, (h + i) % HPC:(h + i) % HPC + 2, 0:keys],
                           start=(i == 0), stop=False)
                    last = mm(dst[:, :, first:first + KEYS0], ident_b[:],
                              hidden[:].unsqueeze(1).to_broadcast([TILE, heads, KEYS0]), start=False, stop=True)
                last.then_inc(smax_mm, 1)

            def turn_max(b):
                turns.take("mixed", b, max_ready, 1, 1)
                pe.wait_ge(max_cols_ready, b.count(1, 1))
                for c in range(2):
                    for j in range(2):
                        last = nc.tensor.transpose(mixed[:, c * PAD + j * TILE:c * PAD + (j + 1) * TILE],
                                                   max_cols[:, 2 * j + c, :], ident[0:TILE, 0:TILE])
                last.then_inc(max_mm, 1)

            def scores(b, s):
                slot = score_slot(b, 5 + s)
                turns.take(("score", slot), b, exp_done, 6, s + 1)
                if s == 0:
                    pe.wait_ge(max_ready, b.count(1, 1))
                for z in range(2):
                    h = 2 * s + z
                    for i, t in enumerate((1, 0)):
                        dst = score[slot][0:TILE, z, i * PAD:(i + 1) * PAD]
                        keys = slice(t * TILE, (t + 1) * TILE)
                        last = mm(dst, k_st[b.par][:, h // HPC, h % HPC, keys], stacked_q(b, h, slice(0, 128)),
                                  start=True, stop=True)
                last.then_inc(score_mm, 1)

            def mix(b, g):
                turns.take("mixed", b, ot_ready, GROUPS, g + 1)
                pe.wait_ge(causal_done, b.count(6, 2 * g + 2))
                if g == 0:
                    pe.wait_ge(v_ready, b.count(1, 1))
                for j in range(4):
                    h = 4 * g + j
                    mm(mixed[32 * j:32 * j + 32, 0:PAD], v_sb[b.par][:, 0, h, :], pt[:, h, KEYS0:PCOLS],
                       start=True, stop=False)
                    last = mm(mixed[32 * j:32 * j + 32, PAD - KEYS0:PAD], v_sb[b.par][:, 1, h, :],
                              pt[:, h, 0:KEYS0], start=False, stop=True)
                last.then_inc(pv_mm, 1)

            def turn_out(c, j):
                name, bank = (("turned", turned), ("mixed", mixed))[j]
                turns.take(name, c, o_ready, 2, j + 1)
                if j == 0:
                    pe.wait_ge(ot_ready, c.count(GROUPS, GROUPS))
                for g in range(GROUPS):
                    last = nc.tensor.transpose(bank[0:TILE, g * 128:(g + 1) * 128],
                                               ot[:, g, j * TILE:(j + 1) * TILE], ident[:])
                last.then_inc(otr_mm, 1)

            def turn_tokens(image, name, bank, src, ready, per, done, read_done):
                turns.take(name, image, read_done, 1, 1)
                pe.wait_ge(ready, image.count(per, per))
                for c in range(2):
                    for j in range(2):
                        last = nc.tensor.transpose(bank[0:HALF, c * PAD + j * TILE:c * PAD + (j + 1) * TILE],
                                                   src[:, j, c * HALF:(c + 1) * HALF], ident[0:TILE, 0:TILE])
                last.then_inc(done, 1)

            def turn_stacked(image, name, bank, src, ready, per, done, read_done):
                turns.take(name, image, read_done, 2, 2)
                pe.wait_ge(ready, image.count(per, per))
                for j in range(2):
                    nc.tensor.transpose(bank[:, j * TILE:(j + 1) * TILE], src[:, j, 0:128], ident[0:TILE, 0:TILE])
                for j in range(2):
                    last = nc.tensor.transpose(bank[:, PAD + j * TILE:PAD + (j + 1) * TILE], src[:, j, 128:256],
                                               ident[0:TILE, 0:TILE])
                last.then_inc(done, 1)

            def patches(a, t):
                turns.take(f"dense{t}", a, h_ready, 2, t + 1)
                pe.wait_ge(x_lo_ready, a.count(2, t + 1))
                tok = slice(t * TILE, (t + 1) * TILE)
                three(dense[t][0:TILE, 0:HID],
                      [(x_hi[:, k, tok], x_lo[:, k, tok], tok_w_hi[:, k, :], tok_w_lo[:, k, :])
                       for k in range(KP)]).then_inc(patch_mm, 1)

            def weights(c, part, first, n):
                return attn_w_sb[:, c, part, first:first + n]

            def qk(a, u):
                turns.take(("dense0", "mixed")[u], a, qk_lo_ready, 2, u + 1)
                if u == 0:
                    pe.wait_ge(xt_lo_ready, a.count(1, 1))
                for half in range(2):
                    first = (HID, 0)[u] + half * HALF
                    last = three((dense[0], mixed)[u][0:HALF, half * PAD:(half + 1) * PAD],
                                 [(weights(c, 0, first, HALF), weights(c, 1, first, HALF), xt_hi[:, c, :], xt_lo[:, c, :])
                                  for c in range(2)])
                last.then_inc(qk_mm, 1)

            def values(a):
                turns.take("turned", a, v_ready, 1, 1)
                for t in range(2):
                    tok = slice(t * TILE, (t + 1) * TILE)
                    last = three(turned[0:TILE, t * HID:(t + 1) * HID],
                                 [(xt_hi[:, c, tok], xt_lo[:, c, tok], weights(c, 0, 2 * HID, HID),
                                   weights(c, 1, 2 * HID, HID)) for c in range(2)])
                last.then_inc(v_mm, 1)

            def project(c):
                turns.take("dense1", c, h2_ready, 1, 1)
                pe.wait_ge(o_lo_ready, c.count(1, 1))
                for j in range(2):
                    tok = slice(j * TILE, (j + 1) * TILE)
                    last = three(dense[1][0:TILE, j * HID:(j + 1) * HID],
                                 [(o_hi[:, k, tok], o_lo[:, k, tok], weights(k, 0, 3 * HID, HID),
                                   weights(k, 1, 3 * HID, HID)) for k in range(2)])
                last.then_inc(proj_mm, 1)

            def gate_sums(c):
                pe.wait_ge(xn2_ready, c.count(3, 2))
                turns.take("turned", c, gsum_ready, 1, 1)
                for k in range(2):
                    for j in range(2):
                        last = mm(turned[0:HALF, k:k + 1], xn2[:, j, k * HALF:(k + 1) * HALF],
                                  real_tok[:, j:j + 1], start=(j == 0), stop=(j == 1))
                last.then_inc(gsum_mm, 1)

            def logits(c):
                pe.wait_ge(gsum_ready, c.count(1, 1))
                turns.take("turned", c, logit_ready, 1, 1)
                for k in range(2):
                    last = mm(turned[0:1, 0:EXPERTS], gate_sum[:, k:k + 1], gate_w_sb[:, k, :],
                              start=(k == 0), stop=(k == 1))
                last.then_inc(logit_mm, 1)

            def spread_weight(c):
                turns.take("turned", c, weight_ready, 1, 1)
                pe.wait_ge(prob_ready, c.count(1, 1))
                mm(turned[0:TILE, 0:1], ones_row[:], gate_prob[:], start=True, stop=True).then_inc(weight_mm, 1)

            def five(dst, act_hi_part, act_lo_part, w, tok, cols, weights_first=False):
                ops = ((act_hi_part[:, 0, tok], 0), (act_hi_part[:, 0, tok], 1), (act_lo_part[:, tok], 0),
                       (act_hi_part[:, 1, tok], 2), (act_hi_part[:, 1, tok], 3))
                for i, (part, block) in enumerate(ops):
                    l, r = (w[:, block, cols], part) if weights_first else (part, w[:, block, cols])
                    last = mm(dst, l, r, start=(i == 0), stop=(i == len(ops) - 1))
                return last

            def up(d, m):
                turns.take(f"dense{UP_BANK[m]}", d, gelu_done, FCH, m + 1)
                if m == 0:
                    pe.wait_ge(w1_in[d.par], d.turns(48, 48))
                    pe.wait_ge(xt2_lo_ready, d.count(2, 2))
                five(dense[UP_BANK[m]][:, 0:PAD], xt2_hi[d.par], xt2_lo[d.par], w1_sb[d.par], slice(0, PAD),
                     slice(m * 128, (m + 1) * 128), weights_first=True).then_inc(up_mm, 1)

            def down(d, j):
                turns.take(f"dense{j}", d, y_ready, 2, j + 1)
                if j == 0:
                    pe.wait_ge(w2_in[d.par], d.turns(32, 32))
                tok = slice(j * TILE, (j + 1) * TILE)
                for m in range(FCH):
                    if j == 0 and m == 0:
                        pe.wait_ge(act_lo0_ready, d.count(1, 1))
                    elif j == 0 and m % 2 == 0:
                        pe.wait_ge(act_lo_ready, d.count(GELU_PAIRS - 1, m // 2))
                    w_hi, w_lo = w2_sb[d.par][:, 0, m, :], w2_sb[d.par][:, 1, m, :]
                    products = ((act_hi, w_hi), (act_hi, w_lo), (act_lo, w_hi))
                    for i, (act_part, w_part) in enumerate(products):
                        last = mm(dense[j][0:TILE, 0:HID], act_part[:, m, tok], w_part,
                                  start=(m == 0 and i == 0), stop=(m == FCH - 1 and i == 2))
                last.then_inc(down_mm, 1)

            def turn(n, trip):
                e, a, b, c, d = (Image(n + k, trip) for k in (2, 1, 0, -1, -2))
                E, A, B, C, D = e.real(), a.real(), b.real(), c.real(), d.real()
                if A:
                    patches(a, 0)
                if C:
                    scores(c, 5)
                    mix(c, 1)
                if A:
                    patches(a, 1)
                if D:
                    spread_weight(d)
                if C:
                    mix(c, 2)
                if B:
                    score_max(b, 0)
                if C:
                    turn_out(c, 0), turn_out(c, 1)
                if B:
                    score_max(b, 1)
                if D:
                    up(d, 0)
                if B:
                    score_max(b, 2)
                if A:
                    turn_tokens(a, "turned", turned, xn, xn_ready, 2, xt_mm, xt_lo_ready)
                if D:
                    up(d, 1)
                if C:
                    turn_tokens(c, "mixed", mixed, o_tok, o_ready, 2, o2_mm, o_lo_ready)
                if B:
                    score_max(b, 3)
                if A:
                    qk(a, 0)
                if B:
                    score_max(b, 4)
                if C:
                    project(c)
                if A:
                    qk(a, 1)
                    values(a)
                if D:
                    up(d, 2), up(d, 3)
                    up(d, 4), up(d, 5)
                if B:
                    turn_max(b)
                if C:
                    gate_sums(c)
                if D:
                    down(d, 0)
                if C:
                    logits(c)
                if B:
                    scores(b, 0)
                    scores(b, 1)
                if C:
                    turn_stacked(c, "mixed", mixed, xn2, xn2_ready, 3, xt2_mm, xt2_lo_ready)
                if D:
                    down(d, 1)
                if B:
                    scores(b, 2), scores(b, 3)
                    mix(b, 0)
                    scores(b, 4)

            def enter(trip):
                turns.trip = trip

            run_turns(pe, turn, enter, turns.leave)


def kernel(x, cls_tok, L0_tok_W_proj, L0_tok_b_proj, L0_attn_w_attn, L0_attn_w_proj, L0_attn_b_proj,
           L0_ffn_Wg, L0_ffn_W1, L0_ffn_b1, L0_ffn_W2, L0_ffn_b2):
    import numpy as np
    import concourse.bacc as bacc
    from concourse.bass_utils import run_bass_kernel_spmd

    cut = np.asarray(x).reshape(IMAGES, GRID, PATCH, GRID, PATCH, CH).transpose(0, 2, 4, 5, 1, 3)
    cols = np.zeros((IMAGES, 128, KP, PAD), np.float32)
    cols[:, :, :, 1:TOKENS] = cut.reshape(IMAGES, 128, KP, GRID * GRID)

    def stack_rows(w):
        return np.ascontiguousarray(np.concatenate([w, w[128:]]).reshape(2, 128, -1).transpose(1, 0, 2))

    arrays = {
        "x_cols": cols,
        "tok_w": np.ascontiguousarray(np.asarray(L0_tok_W_proj).reshape(128, KP, HID)),
        "tok_bias": np.asarray(L0_tok_b_proj),
        "attn_w": np.concatenate([np.asarray(L0_attn_w_attn), np.asarray(L0_attn_w_proj)], axis=1),
        "proj_bias": np.asarray(L0_attn_b_proj),
        "cls": np.asarray(cls_tok).reshape(1, HID),
        "gate_w": np.ascontiguousarray(np.asarray(L0_ffn_Wg).reshape(EXPERTS, 2, HALF).transpose(2, 1, 0)),
        "w1": np.stack([stack_rows(w) for w in np.asarray(L0_ffn_W1)]),
        "w2": np.ascontiguousarray(
            np.asarray(L0_ffn_W2).reshape(EXPERTS, FCH, 128, HID).transpose(0, 2, 1, 3).reshape(EXPERTS, 128, FCH * HID)),
        "b1": np.ascontiguousarray(np.asarray(L0_ffn_b1).reshape(EXPERTS, FCH, 128).transpose(0, 2, 1)),
        "b2": np.asarray(L0_ffn_b2),
    }
    nc = bacc.Bacc("TRN2", target_bir_lowering=False, num_devices=1)
    aps = {k: nc.dram_tensor(k, v.shape, F32, kind="ExternalInput").ap() for k, v in arrays.items()}
    out = nc.dram_tensor("out", (IMAGES, TOKENS, HID), F32, kind="ExternalOutput").ap()
    vit_tower(nc, aps["x_cols"], aps["tok_w"], aps["tok_bias"], aps["attn_w"], aps["proj_bias"],
              aps["cls"], aps["gate_w"], aps["w1"], aps["w2"], aps["b1"], aps["b2"], out)
    result = run_bass_kernel_spmd(nc, [arrays], core_ids=[0])
    return result.results[0]["out"]
```
